# Optimizing a Trainium2 kernel written in Bass

```python
import numpy as np
import jax
import jax.numpy as jnp

def _softmax(x, axis=-1):
    return jax.nn.softmax(x, axis=axis)

def _gelu(x):
    return jax.nn.gelu(x, approximate=True)

def _silu(x):
    return jax.nn.silu(x)

def _sigmoid(x):
    return jax.nn.sigmoid(x)

def _layernorm(x, axis=-1, eps=1e-05):
    m = jnp.mean(x, axis=axis, keepdims=True)
    v = jnp.var(x, axis=axis, keepdims=True)
    return (x - m) / jnp.sqrt(v + eps)

def _scatter_add(tgt, idx, src, axis=0):
    return tgt.at[idx].add(src)

def _segment_sum(src, seg, n):
    return jax.ops.segment_sum(src, seg, n)
kernel_name = 'mk_seq_preln_d1_jaxref_r4_a655c6'

def setup_inputs(seed: int=0):
    np.random.seed(seed)
    _w = jnp.asarray

    def _L0_attn_setup():
        import jax, jax.numpy as jnp
        import numpy as np
        DIM = 512
        HEAD_DIM = 128
        NH = DIM // HEAD_DIM
        CHUNK = 128

        def _forward(x, Wq, bq, Wk, bk, Wv, bv, Wbeta, bbeta, Walpha, balpha):
            B, T, D = x.shape
            H, S, C = (NH, HEAD_DIM, CHUNK)
            q = (x @ Wq + bq).reshape(B, T, H, S)
            k = (x @ Wk + bk).reshape(B, T, H, S)
            v = (x @ Wv + bv).reshape(B, T, H, S)
            k = k / jnp.maximum(jnp.linalg.norm(k, axis=-1, keepdims=True), 1e-12)
            alpha_val = jax.nn.sigmoid(x @ Walpha + balpha).reshape(B, T, H, 1)
            beta = jax.nn.softplus(x @ Wbeta + bbeta).reshape(B, T, H, 1)
            pad = -T % C

            def padt(t):
                return jnp.pad(t, ((0, 0), (0, pad), (0, 0), (0, 0))) if pad else t
            qp, kp, vp = (padt(q), padt(k), padt(v))
            ap, bp = (padt(alpha_val), padt(beta))
            Tp = T + pad
            n = Tp // C

            def ch(t):
                return t.reshape(B, n, C, H, t.shape[-1]).transpose(0, 1, 3, 2, 4)
            qc, kc, vc, bc = (ch(qp), ch(kp), ch(vp), ch(bp))
            cla = jnp.cumsum(jnp.log(ch(ap) + 1e-06), axis=3)
            decay = jnp.exp(cla - jnp.swapaxes(cla, -1, -2))
            causal = jnp.tril(jnp.ones((C, C), dtype=bool))
            decay = jnp.where(causal, decay, 0.0)
            attn = jnp.einsum('bnhcd,bnhed->bnhce', qc, kc) * jnp.swapaxes(bc, -1, -2) * decay
            y_local = jnp.einsum('bnhce,bnhed->bnhcd', attn, vc)
            chunk_decay = jnp.exp(cla)
            cla_end = cla[:, :, :, -1:, :]
            total_decay = jnp.exp(cla_end)
            decay_to_end = jnp.exp(cla_end - cla)
            kw = kc * bc * decay_to_end
            delta = jnp.einsum('bnhcd,bnhce->bnhde', vc, kw)
            state0 = jnp.zeros((B, H, S, S), x.dtype)

            def step(state, inp):
                q_i, yloc_i, cd_i, td_i, d_i = inp
                y_glob = jnp.einsum('bhce,bhde->bhcd', q_i, state) * cd_i
                new_state = state * td_i + d_i
                return (new_state, y_glob + yloc_i)
            xs = (jnp.moveaxis(qc, 1, 0), jnp.moveaxis(y_local, 1, 0), jnp.moveaxis(chunk_decay, 1, 0), jnp.moveaxis(total_decay, 1, 0), jnp.moveaxis(delta, 1, 0))
            final_state, y_chunks = jax.lax.scan(step, state0, xs)
            y = jnp.moveaxis(y_chunks, 0, 1)
            y = y.transpose(0, 1, 3, 2, 4).reshape(B, Tp, D)[:, :T, :]
            surprise = jnp.linalg.norm(y_local, axis=-1).mean(axis=-1)
            surprise = surprise.reshape(B, -1, 1).mean(axis=1, keepdims=True)
            return (y, final_state, surprise, alpha_val)

        def _reference_tuple_inner(x, Wq, bq, Wk, bk, Wv, bv, Wbeta, bbeta, Walpha, balpha):
            return _forward(x, Wq, bq, Wk, bk, Wv, bv, Wbeta, bbeta, Walpha, balpha)
        key = jax.random.key(seed)
        ks = jax.random.split(key, 6)
        B, T = (2, 1024)
        s = 1.0 / np.sqrt(DIM)

        def lin(k, out_dim):
            k1, k2 = jax.random.split(k)
            W = jax.random.uniform(k1, (DIM, out_dim), minval=-s, maxval=s, dtype=jnp.float32)
            b = jax.random.uniform(k2, (out_dim,), minval=-s, maxval=s, dtype=jnp.float32)
            return (W, b)
        Wq, bq = lin(ks[0], NH * HEAD_DIM)
        Wk, bk = lin(ks[1], NH * HEAD_DIM)
        Wv, bv = lin(ks[2], NH * HEAD_DIM)
        Wbeta, bbeta = lin(ks[3], NH)
        Walpha, _ = lin(ks[4], NH)
        balpha = jnp.full((NH,), 2.0, dtype=jnp.float32)
        x = jax.random.normal(ks[5], (B, T, DIM), dtype=jnp.float32)
        return {'x': x, 'Wq': Wq, 'bq': bq, 'Wk': Wk, 'bk': bk, 'Wv': Wv, 'bv': bv, 'Wbeta': Wbeta, 'bbeta': bbeta, 'Walpha': Walpha, 'balpha': balpha}
    _L0_attn_in = _L0_attn_setup()

    def _L0_ffn_setup():
        import jax, jax.numpy as jnp
        import numpy as np
        BLOCK_SIZE = 32
        HIDDEN_SIZE = 512
        MLP_DIM = 4096
        NVFP4_LUT = jnp.array([0.0, 0.5, 1.0, 1.5, 2.0, 3.0, 4.0, 6.0, 0.0, -0.5, -1.0, -1.5, -2.0, -3.0, -4.0, -6.0], dtype=jnp.float32)

        def dequant_nvfp4(W_packed, scales, block=BLOCK_SIZE):
            N = W_packed.shape[0]
            low = W_packed & 15
            high = W_packed >> 4 & 15
            idx = jnp.stack([low, high], axis=-1).reshape(N, -1)
            vals = NVFP4_LUT[idx]
            K = vals.shape[1]
            vals = vals.reshape(N, K // block, block) * scales[:, :, None]
            return vals.reshape(N, K)
        key = jax.random.key(seed)
        ks = jax.random.split(key, 7)
        x = jax.random.normal(ks[0], (4, 32, HIDDEN_SIZE), dtype=jnp.float32)
        gate_W_packed = jax.random.randint(ks[1], (MLP_DIM, HIDDEN_SIZE // 2), 0, 64, dtype=jnp.int32)
        gate_scales = jax.random.uniform(ks[2], (MLP_DIM, HIDDEN_SIZE // BLOCK_SIZE), dtype=jnp.float32) * 0.1 + 0.001
        up_W_packed = jax.random.randint(ks[3], (MLP_DIM, HIDDEN_SIZE // 2), 0, 64, dtype=jnp.int32)
        up_scales = jax.random.uniform(ks[4], (MLP_DIM, HIDDEN_SIZE // BLOCK_SIZE), dtype=jnp.float32) * 0.1 + 0.001
        down_W_packed = jax.random.randint(ks[5], (HIDDEN_SIZE, MLP_DIM // 2), 0, 64, dtype=jnp.int32)
        down_scales = jax.random.uniform(ks[6], (HIDDEN_SIZE, MLP_DIM // BLOCK_SIZE), dtype=jnp.float32) * 0.1 + 0.001
        return {'x': x, 'gate_W_packed': gate_W_packed, 'gate_scales': gate_scales, 'up_W_packed': up_W_packed, 'up_scales': up_scales, 'down_W_packed': down_W_packed, 'down_scales': down_scales}
    _L0_ffn_in = _L0_ffn_setup()
    _d = {'L0_attn_x': _L0_attn_in['x'], 'L0_attn_Wq': _L0_attn_in['Wq'], 'L0_attn_bq': _L0_attn_in['bq'], 'L0_attn_Wk': _L0_attn_in['Wk'], 'L0_attn_bk': _L0_attn_in['bk'], 'L0_attn_Wv': _L0_attn_in['Wv'], 'L0_attn_bv': _L0_attn_in['bv'], 'L0_attn_Wbeta': _L0_attn_in['Wbeta'], 'L0_attn_bbeta': _L0_attn_in['bbeta'], 'L0_attn_Walpha': _L0_attn_in['Walpha'], 'L0_attn_balpha': _L0_attn_in['balpha'], 'L0_ffn_gate_W_packed': _L0_ffn_in['gate_W_packed'], 'L0_ffn_gate_scales': _L0_ffn_in['gate_scales'], 'L0_ffn_up_W_packed': _L0_ffn_in['up_W_packed'], 'L0_ffn_up_scales': _L0_ffn_in['up_scales'], 'L0_ffn_down_W_packed': _L0_ffn_in['down_W_packed'], 'L0_ffn_down_scales': _L0_ffn_in['down_scales']}
    _x0 = _d['L0_attn_x']
    _d['L0_attn_x'] = jax.random.normal(jax.random.fold_in(jax.random.key(seed), 1), (4, 512, 512), dtype=_x0.dtype)
    del _x0
    return _d

def reference(L0_attn_x, L0_attn_Wq, L0_attn_bq, L0_attn_Wk, L0_attn_bk, L0_attn_Wv, L0_attn_bv, L0_attn_Wbeta, L0_attn_bbeta, L0_attn_Walpha, L0_attn_balpha, L0_ffn_gate_W_packed, L0_ffn_gate_scales, L0_ffn_up_W_packed, L0_ffn_up_scales, L0_ffn_down_W_packed, L0_ffn_down_scales):

    def _L0_attn_ref(x, Wq, bq, Wk, bk, Wv, bv, Wbeta, bbeta, Walpha, balpha):
        import jax, jax.numpy as jnp
        import numpy as np
        DIM = 512
        HEAD_DIM = 128
        NH = DIM // HEAD_DIM
        CHUNK = 128

        def _forward(x, Wq, bq, Wk, bk, Wv, bv, Wbeta, bbeta, Walpha, balpha):
            B, T, D = x.shape
            H, S, C = (NH, HEAD_DIM, CHUNK)
            q = (x @ Wq + bq).reshape(B, T, H, S)
            k = (x @ Wk + bk).reshape(B, T, H, S)
            v = (x @ Wv + bv).reshape(B, T, H, S)
            k = k / jnp.maximum(jnp.linalg.norm(k, axis=-1, keepdims=True), 1e-12)
            alpha_val = jax.nn.sigmoid(x @ Walpha + balpha).reshape(B, T, H, 1)
            beta = jax.nn.softplus(x @ Wbeta + bbeta).reshape(B, T, H, 1)
            pad = -T % C

            def padt(t):
                return jnp.pad(t, ((0, 0), (0, pad), (0, 0), (0, 0))) if pad else t
            qp, kp, vp = (padt(q), padt(k), padt(v))
            ap, bp = (padt(alpha_val), padt(beta))
            Tp = T + pad
            n = Tp // C

            def ch(t):
                return t.reshape(B, n, C, H, t.shape[-1]).transpose(0, 1, 3, 2, 4)
            qc, kc, vc, bc = (ch(qp), ch(kp), ch(vp), ch(bp))
            cla = jnp.cumsum(jnp.log(ch(ap) + 1e-06), axis=3)
            decay = jnp.exp(cla - jnp.swapaxes(cla, -1, -2))
            causal = jnp.tril(jnp.ones((C, C), dtype=bool))
            decay = jnp.where(causal, decay, 0.0)
            attn = jnp.einsum('bnhcd,bnhed->bnhce', qc, kc) * jnp.swapaxes(bc, -1, -2) * decay
            y_local = jnp.einsum('bnhce,bnhed->bnhcd', attn, vc)
            chunk_decay = jnp.exp(cla)
            cla_end = cla[:, :, :, -1:, :]
            total_decay = jnp.exp(cla_end)
            decay_to_end = jnp.exp(cla_end - cla)
            kw = kc * bc * decay_to_end
            delta = jnp.einsum('bnhcd,bnhce->bnhde', vc, kw)
            state0 = jnp.zeros((B, H, S, S), x.dtype)

            def step(state, inp):
                q_i, yloc_i, cd_i, td_i, d_i = inp
                y_glob = jnp.einsum('bhce,bhde->bhcd', q_i, state) * cd_i
                new_state = state * td_i + d_i
                return (new_state, y_glob + yloc_i)
            xs = (jnp.moveaxis(qc, 1, 0), jnp.moveaxis(y_local, 1, 0), jnp.moveaxis(chunk_decay, 1, 0), jnp.moveaxis(total_decay, 1, 0), jnp.moveaxis(delta, 1, 0))
            final_state, y_chunks = jax.lax.scan(step, state0, xs)
            y = jnp.moveaxis(y_chunks, 0, 1)
            y = y.transpose(0, 1, 3, 2, 4).reshape(B, Tp, D)[:, :T, :]
            surprise = jnp.linalg.norm(y_local, axis=-1).mean(axis=-1)
            surprise = surprise.reshape(B, -1, 1).mean(axis=1, keepdims=True)
            return (y, final_state, surprise, alpha_val)

        def _reference_tuple_inner(x, Wq, bq, Wk, bk, Wv, bv, Wbeta, bbeta, Walpha, balpha):
            return _forward(x, Wq, bq, Wk, bk, Wv, bv, Wbeta, bbeta, Walpha, balpha)
        return _reference_tuple_inner(x, Wq, bq, Wk, bk, Wv, bv, Wbeta, bbeta, Walpha, balpha)[0]

    def _L0_ffn_ref(x, gate_W_packed, gate_scales, up_W_packed, up_scales, down_W_packed, down_scales):
        import jax, jax.numpy as jnp
        import numpy as np
        BLOCK_SIZE = 32
        HIDDEN_SIZE = 512
        MLP_DIM = 4096
        NVFP4_LUT = jnp.array([0.0, 0.5, 1.0, 1.5, 2.0, 3.0, 4.0, 6.0, 0.0, -0.5, -1.0, -1.5, -2.0, -3.0, -4.0, -6.0], dtype=jnp.float32)

        def dequant_nvfp4(W_packed, scales, block=BLOCK_SIZE):
            N = W_packed.shape[0]
            low = W_packed & 15
            high = W_packed >> 4 & 15
            idx = jnp.stack([low, high], axis=-1).reshape(N, -1)
            vals = NVFP4_LUT[idx]
            K = vals.shape[1]
            vals = vals.reshape(N, K // block, block) * scales[:, :, None]
            return vals.reshape(N, K)
        B, S, H = x.shape
        xt = x.reshape(B * S, H)
        Wg = dequant_nvfp4(gate_W_packed, gate_scales)
        Wu = dequant_nvfp4(up_W_packed, up_scales)
        Wd = dequant_nvfp4(down_W_packed, down_scales)
        gate = jnp.einsum('th,nh->tn', xt, Wg)
        up = jnp.einsum('th,nh->tn', xt, Wu)
        gelu = jnp.tanh(0.7978845608028654 * (gate + 0.044715 * gate ** 3)) * gate * 0.5 + gate * 0.5
        inter = gelu * up
        out = jnp.einsum('tn,hn->th', inter, Wd)
        return out.reshape(B, S, H)
    x = L0_attn_x
    x = x + _L0_attn_ref(_layernorm(x, axis=-1), L0_attn_Wq, L0_attn_bq, L0_attn_Wk, L0_attn_bk, L0_attn_Wv, L0_attn_bv, L0_attn_Wbeta, L0_attn_bbeta, L0_attn_Walpha, L0_attn_balpha)
    x = x + _L0_ffn_ref(_layernorm(x, axis=-1), L0_ffn_gate_W_packed, L0_ffn_gate_scales, L0_ffn_up_W_packed, L0_ffn_up_scales, L0_ffn_down_W_packed, L0_ffn_down_scales)
    return x

_drawn_inputs = setup_inputs


def setup_inputs(seed=0):
    import zlib

    import numpy as np

    out = dict(_drawn_inputs(seed))
    spreads = {'L0_attn_balpha': (2.0, 0.2)}
    factors = {'L0_attn_bbeta': 6.467}
    for name, (base, spread) in spreads.items():
        noise = np.random.default_rng([zlib.crc32(name.encode()), seed]).standard_normal(out[name].shape)
        drawn = base * np.exp(spread * noise) if base else spread * noise
        out[name] = jnp.asarray(drawn.astype(out[name].dtype))
    for name, factor in factors.items():
        out[name] = (out[name] * factor).astype(out[name].dtype)
    return out
```

```python
from contextlib import ExitStack

import concourse.bass as bass
from concourse import mybir

F32 = mybir.dt.float32
F16 = mybir.dt.float16
I32 = mybir.dt.int32
ALU = mybir.AluOpType
ACT = mybir.ActivationFunctionType

NT = 16
NG = 8
NI = NG * 16

XS = 2.0 ** 11
QS = 2.0 ** 10
WS = 2.0 ** 10
IS = 2.0 ** -2
CODE = WS * 2.0 ** 14
GK = 0.7978845608028654
CUB = 0.044715


class Lane:

    def __init__(self, marks, sem):
        self.marks, self.sem, self.items, self.count = marks, sem, [], 0

    def do(self, fn, mark=None):
        if mark is not None:
            self.count += 1
            assert mark not in self.marks, mark
            self.marks[mark] = (self.sem, self.count)
        self.items.append((fn, mark))

    def load(self, fn, mark, sem, value):
        self.marks[mark] = (sem, value)
        self.items.append((fn, (sem,)))

    def need(self, *names):
        self.items.append((None, names))

    def emit(self, eng):
        seen = {}
        for fn, x in self.items:
            if fn is None:
                for name in x:
                    sem, value = self.marks[name]
                    if seen.get(sem.name, 0) < value:
                        eng.wait_ge(sem, value)
                        seen[sem.name] = value
                continue
            ins = fn(eng)
            if isinstance(x, tuple) and len(x) == 1 and not isinstance(x[0], str):
                ins.then_inc(x[0], 16)
            elif x is not None:
                ins.then_inc(self.sem, 1)


def block_kernel(nc, x, wqkv, bqk, bv, wab, bab, codes, scales, out):
    with ExitStack() as ctx:
        def sb(name, shape, dt):
            return ctx.enter_context(nc.sbuf_tensor(name, shape, dt))

        def sem(name):
            return ctx.enter_context(nc.semaphore(name))

        X1 = sb("X1", [128, NT, 512], F32)
        XT = sb("XT", [128, 2, 4, NT * 128], F16)
        WR0 = sb("WR0", [128, 2, 12, 512], F16)
        WR1 = sb("WR1", [128, 2, 12, 512], F16)
        REG = sb("REG", [128, 3, 2, 2048], F32)
        raw = sb("raw", [128, 3, 512], I32)
        scl = sb("scl", [128, 3, 512], F32)
        tb = sb("tb", [128, 512], I32)
        ub = sb("ub", [128, 512], I32)
        wf = sb("wf", [128, 2, 512], F32)
        xh = sb("xh", [128, 2, 512], F32)
        dec = sb("dec", [128, 2, 512], F32)
        att = sb("att", [128, 1, 512], F32)
        kwb = sb("kwb", [128, 1, 512], F32)
        lau = sb("lau", [128, 1, 512], F32)
        st = sb("st", [128, 2, 512], F32)
        junk = sb("junk", [128, 512], mybir.dt.bfloat16)
        ident = sb("ident", [128, 128], F32)
        upper = sb("upper", [128, 128], F32)
        lower = sb("lower", [128, 128], F32)
        ones = sb("ones", [128, 128], F32)
        bvb = sb("bvb", [128, 512], F32)
        babb = sb("babb", [128, 8], F32)
        bqk_s = sb("bqk_s", [128, 8], F32)
        wab_f = sb("wab_f", [128, 4, 8], F32)
        wab_h = sb("wab_h", [128, 2, 4, 8], F16)
        z = sb("z", [128, NT, 8], F32)
        sm = sb("sm", [128, 9, 64], F32)
        bst = sb("bst", [128, 2, 6], F32)
        mv = sb("mv", [128, 2, 2], F32)
        rs = sb("rs", [128, 2, 2], F32)
        half = sb("half", [128, 4], F32)
        kn_s = sb("kn_s", [128, 2, 5, 4], F32)

        WR = [WR0, WR1]
        wq = WR1[:, :, :, :].rearrange("p a m n -> p (a m n)").rearrange("p (a k n) -> p a k n", a=2, k=4)
        qT = REG[:, 0, :, :].rearrange("p b (h t) -> p b h t", h=4)
        kT = REG[:, 1, :, :].rearrange("p b (h t) -> p b h t", h=4)
        vv = REG[:, 2, :, :].rearrange("p b (i d) -> p b i d", i=4)
        wst = REG[:, 1, :, :].rearrange("p b n -> p (b n)")
        wst2 = REG[:, 2, 0, :]
        fr = REG[:, :, :, :].rearrange("p a b n -> p (a b n)").rearrange("p (m n) -> p m n", n=512)
        sq = [fr[:, 0, :], fr[:, 1, :]]
        pb = [fr[:, 2, :], fr[:, 3, :]]
        tnh = [fr[:, 4, :], fr[:, 5, :]]
        wgb = [fr[:, 6, :], fr[:, 7, :]]
        inf = [fr[:, 8, :], fr[:, 9, :]]
        ihl = fr[:, 10:14, :].bitcast(F16).rearrange("p s (a t) -> p s a t", a=2)

        PS = [ctx.enter_context(nc.psum_tensor(f"ps{i}", [128, 512], F32)) for i in range(8)]

        s_pe, s_act, s_dve, s_pool = sem("s_pe"), sem("s_act"), sem("s_dve"), sem("s_pool")
        s_x = [sem(f"s_x{b}") for b in range(4)]
        s_w = [sem(f"s_w{k}") for k in range(4)]
        s_c = sem("s_c")
        s_d = [sem(f"s_d{k}") for k in range(3)]
        s_o = sem("s_o")

        marks = {}
        PE, AC, DV, PL = (Lane(marks, s) for s in (s_pe, s_act, s_dve, s_pool))
        SP = Lane(marks, None)

        def h4(ap):
            return ap.rearrange("p (h t) -> p h t", h=4)

        xv = x.rearrange("(b i p) d -> b p i d", b=4, p=128)
        wv = wqkv.rearrange("(k p) n -> k p n", p=128)
        for b in range(4):
            SP.load(lambda e, b=b: e.dma_start(X1[:, 4 * b:4 * b + 4, :], xv[b]), ("x", b), s_x[b], 16)
            if b == 0:
                small = [
                    lambda e: e.dma_start(bqk_s[:, :], bqk),
                    lambda e: e.dma_start(bvb[:, :], bv.broadcast_to([128, 512])),
                    lambda e: e.dma_start(babb[:, :], bab.broadcast_to([128, 8])),
                    lambda e: e.dma_start(wab_f[:, :, :], wab.rearrange("(k p) n -> p k n", p=128)),
                ]
                for f in small:
                    SP.load(f, ("consts",), s_c, 64)
            k = b
            dst = wst[:, 1536 * k:1536 * k + 1536] if k < 2 else (wst2[:, 0:1536] if k == 2 else
                                                              REG[:, 2, 1, 0:1536])
            SP.load(lambda e, k=k, dst=dst: e.dma_start(dst, wv[k]), ("w", k), s_w[k], 16)
        wsrc = [wst[:, 0:1536], wst[:, 1536:3072], wst2[:, 0:1536], REG[:, 2, 1, 0:1536]]

        def load_chunk(k):
            s = k % 3
            if k >= 3:
                SP.need(("wf", k - 3, 1))
            SP.load(lambda e: e.dma_start(raw[:, s, :], codes[k // 6, k % 6]), ("raw", k), s_d[s], 32 * (k // 3 + 1))
            src = scales[k // 6, k % 6]
            rep = bass.AP(src.tensor, src.offset, [[512, 8], [0, 16], [1, 512]])
            SP.load(lambda e: e.dma_start(scl[:, s, :], rep), ("scl", k), s_d[s], 32 * (k // 3 + 1))

        PL.do(lambda e: e.memset(ident[:, :], 0.0), "z0")
        PL.do(lambda e: e.memset(ones[:, :], 1.0), "ones")
        PL.do(lambda e: e.memset(half[:, :], -0.5), "half")
        PL.need("half")
        PL.do(lambda e: e.affine_select(out=ident[:, :], in_=ident[:, :], compare_op=ALU.not_equal, fill=1.0,
                                        base=0, pattern=[[-1, 128]], channel_multiplier=1), "ident")
        PL.do(lambda e: e.affine_select(out=upper[:, :], in_=ones[:, :], compare_op=ALU.is_ge, fill=0.0,
                                        base=0, pattern=[[1, 128]], channel_multiplier=-1), "upper")
        PL.do(lambda e: e.affine_select(out=lower[:, :], in_=ones[:, :], compare_op=ALU.is_gt, fill=0.0,
                                        base=0, pattern=[[-1, 128]], channel_multiplier=1), "lower")

        ring = []

        def ring_take():
            r = len(ring)
            if r >= 2:
                PE.need(ring[r - 2])
            ring.append(None)
            return r, PS[r % 2]

        def norm_stats(tag, T, xt, pre):
            s = T % 2
            DV.need(*pre)
            DV.do(lambda e: e.bn_stats(bst[:, s, :], xt), (tag, "bs", T))
            DV.need((tag, "bs", T))
            DV.do(lambda e: e.bn_aggr(mv[:, s, :], bst[:, s, :]), (tag, "mv", T))
            PL.need((tag, "mv", T))
            PL.do(lambda e: e.tensor_scalar(rs[:, s, 0:1], mv[:, s, 1:2], 1e-5, XS ** -2, ALU.add, ALU.mult),
                  (tag, "ve", T))
            PL.need((tag, "ve", T))
            PL.do(lambda e: e.tensor_tensor(rs[:, s, 1:2], rs[:, s, 0:1], half[:, 0:1], ALU.pow), (tag, "rs", T))

        def norm_apply(tag, T, xt, war):
            s = T % 2
            DV.need((tag, "rs", T), *war)
            DV.do(lambda e: e.tensor_scalar(xh[:, s, :], xt, mv[:, s, 0:1], rs[:, s, 1:2], ALU.subtract, ALU.mult),
                  (tag, "xh", T))

        def turn(tag, T, strided):
            s = T % 2
            PE.need((tag, "xh", T))
            if tag == "n1" and T == 0:
                PE.need("ident")
            r, bank = ring_take()
            for kt in range(4):
                if strided:
                    src = xh[:, s, 256 * (kt // 2) + kt % 2:256 * (kt // 2) + 256:2]
                else:
                    src = xh[:, s, 128 * kt:128 * kt + 128]
                PE.do(lambda e, kt=kt, src=src: e.transpose(bank[:, 128 * kt:128 * kt + 128], src, ident[:, :]),
                      (tag, "t", T) if kt == 3 else None)
            ring[r] = (tag, "lo", T)
            hi = XT[:, 0, :, 128 * T:128 * T + 128]
            lo = XT[:, 1, :, 128 * T:128 * T + 128]
            AC.need((tag, "t", T))
            AC.do(lambda e: e.copy(hi, h4(bank[:, :])), (tag, "hi", T))
            DV.need((tag, "hi", T))
            DV.do(lambda e: e.tensor_tensor(lo, h4(bank[:, :]), hi, ALU.subtract), (tag, "lo", T))

        XP = [(0, 0), (1, 0), (0, 1)]

        def logits(T):
            PE.need(("n1", "hi", T), ("n1", "lo", T), "wab")
            n = 0
            for kt in range(4):
                for xp, wp in XP:
                    PE.do(lambda e, kt=kt, xp=xp, wp=wp, n=n: e.matmul(
                        PS[2][:, 8 * T:8 * T + 8], XT[:, xp, kt, 128 * T:128 * T + 128], wab_h[:, wp, kt, :],
                        start=(n == 0), stop=(n == 11)), ("lg", T) if n == 11 else None)
                    n += 1

        DV.need(("consts",))
        AC.need(("consts",))
        AC.do(lambda e: e.mul(wab_h[:, 0, :, :], wab_f[:, :, :], QS), "wab_hi")
        DV.need("wab_hi")
        DV.do(lambda e: e.scalar_tensor_tensor(wab_h[:, 1, :, :], wab_f[:, :, :], QS, wab_h[:, 0, :, :],
                                               ALU.mult, ALU.subtract), "wab")

        def wprep(k):
            AC.need(("w", k))
            DV.need(("w", k))
            for j in range(3):
                src = wsrc[k][:, 512 * j:512 * j + 512]
                hi = wq[:, 0, k, 512 * j:512 * j + 512]
                lo = wq[:, 1, k, 512 * j:512 * j + 512]
                AC.do(lambda e, hi=hi, src=src: e.mul(hi, src, QS), ("wqh", k, j))
                DV.need(("wqh", k, j))
                DV.do(lambda e, hi=hi, lo=lo, src=src: e.scalar_tensor_tensor(lo, src, QS, hi, ALU.mult, ALU.subtract),
                      ("wql", k, j))

        def dq_bits(k):
            s = k % 3
            DV.need(("raw", k), ("scl", k))
            DV.do(lambda e: e.scalar_tensor_tensor(tb[:, :], raw[:, s, :], 12, raw[:, s, :],
                                                   ALU.logical_shift_left, ALU.bitwise_or), ("dt", k))
            DV.need(("dt", k))
            DV.do(lambda e: e.tensor_scalar(ub[:, :], tb[:, :], 9, 0x0E000E00, ALU.logical_shift_left,
                                            ALU.bitwise_and), ("du", k))
            DV.do(lambda e: e.tensor_scalar(tb[:, :], tb[:, :], 12, -0x7FFF8000, ALU.logical_shift_left,
                                            ALU.bitwise_and), ("dv", k))
            DV.need(("dv", k))
            DV.do(lambda e: e.tensor_tensor(ub[:, :], ub[:, :], tb[:, :], ALU.bitwise_or), ("dw", k))

        u16 = ub[:, :].bitcast(F16)

        def dq_mul(k):
            s, g, c = k % 3, k // 6, k % 6
            DV.need(("dw", k))
            for nib in range(2):
                if k >= 1:
                    DV.need(("wlo", k - 1, nib))
                DV.do(lambda e, nib=nib: e.scalar_tensor_tensor(wf[:, nib, :], u16[:, nib::2], CODE, scl[:, s, :],
                                                                ALU.mult, ALU.mult), ("wf", k, nib))
                buf, m = WR[g % 2], 2 * c + nib
                AC.need(("wf", k, nib))
                if g == 1:
                    AC.need("qkv_done")
                if g >= 2:
                    AC.need(("dn", 16 * (g - 1) - 1))
                AC.do(lambda e, nib=nib, buf=buf, m=m: e.copy(buf[:, 0, m, :], wf[:, nib, :]), ("whi", k, nib))
                PL.need(("whi", k, nib))
                PL.do(lambda e, nib=nib, buf=buf, m=m: e.tensor_tensor(buf[:, 1, m, :], wf[:, nib, :], buf[:, 0, m, :],
                                                                      ALU.subtract), ("wlo", k, nib))

        def qkv(b, kind, h):
            for T in range(4 * b, 4 * b + 4):
                PE.need(("n1", "hi", T), ("n1", "lo", T))
            for k in range(4):
                for j in range(3):
                    PE.need(("wqh", k, j), ("wql", k, j))
            r, bank = ring_take()
            n = 0
            for kt in range(4):
                for xp, wp in XP:
                    xs = XT[:, xp, kt, 512 * b:512 * b + 512]
                    if kind == "v":
                        lhs, rhs = xs[:, 128 * h:128 * h + 128], wq[:, wp, kt, 1024:1536]
                    else:
                        o = (0 if kind == "q" else 512) + 128 * h
                        lhs, rhs = wq[:, wp, kt, o:o + 128], xs
                    PE.do(lambda e, lhs=lhs, rhs=rhs, n=n: e.matmul(bank[:, :], lhs, rhs, start=(n == 0), stop=(n == 11)),
                          (kind, "mm", b, h) if n == 11 else None)
                    n += 1
            ring[r] = (kind, b, h)
            f = 1.0 / (XS * QS)
            if kind == "v":
                DV.need((kind, "mm", b, h))
                DV.do(lambda e: e.scalar_tensor_tensor(vv[:, b % 2, h, :], bank[:, :], f, bvb[:, :], ALU.mult, ALU.add),
                      (kind, b, h))
            elif kind == "q":
                AC.need((kind, "mm", b, h))
                AC.do(lambda e: e.activation(qT[:, b % 2, h, :], bank[:, :], ACT.Identity, bias=bqk_s[:, h:h + 1],
                                             scale=f), (kind, b, h))
            else:
                DV.need((kind, "mm", b, h))
                DV.do(lambda e: e.tensor_scalar(kT[:, b % 2, h, :], bank[:, :], f, bqk_s[:, 4 + h:5 + h],
                                                ALU.mult, ALU.add), (kind, b, h))

        QKV = [(k, h) for h in range(4) for k in "kqv"]

        def gates():
            zl = PS[2][:, 0:128].rearrange("p (t g) -> p t g", g=8)
            DV.need(("lg", NT - 1))
            DV.do(lambda e: e.scalar_tensor_tensor(
                z[:, :, :], zl, 1.0 / (XS * QS), babb[:, :].unsqueeze(1).broadcast_to([128, NT, 8]),
                ALU.mult, ALU.add), "z")
            za, zb = z[:, :, 0:4], z[:, :, 4:8]

            def S(i):
                return sm[:, i, :].rearrange("p (t h) -> p t h", h=4)

            DV.need("z")
            DV.do(lambda e: e.tensor_scalar(S(0), za, -1.0, 80.0, ALU.mult, ALU.min), "g0")
            DV.do(lambda e: e.scalar_tensor_tensor(S(1), zb, -1.0, zb, ALU.mult, ALU.min), "g1")
            AC.need("g1")
            AC.do(lambda e: e.activation(sm[:, 0, :], sm[:, 0, :], ACT.Exp), "g2")
            AC.do(lambda e: e.activation(sm[:, 1, :], sm[:, 1, :], ACT.Exp), "g3")
            DV.need("g3")
            DV.do(lambda e: e.tensor_scalar(sm[:, 0, :], sm[:, 0, :], 1.0, None, ALU.add), "g4")
            DV.do(lambda e: e.tensor_scalar(sm[:, 2, :], sm[:, 1, :], 1.0, None, ALU.add), "g5")
            DV.need("g5")
            DV.do(lambda e: e.reciprocal(sm[:, 0, :], sm[:, 0, :]), "g6")
            DV.do(lambda e: e.tensor_scalar(sm[:, 3, :], sm[:, 2, :], -1.0, None, ALU.add), "g7")
            DV.need("g7")
            DV.do(lambda e: e.tensor_scalar(sm[:, 0, :], sm[:, 0, :], 1e-6, None, ALU.add), "g8")
            DV.do(lambda e: e.tensor_scalar(sm[:, 4, :], sm[:, 3, :], 0.0, None, ALU.is_equal), "g9")
            DV.do(lambda e: e.tensor_scalar(sm[:, 3, :], sm[:, 3, :], 1e-9, None, ALU.max), "g10")
            DV.need("g10")
            DV.do(lambda e: e.reciprocal(sm[:, 3, :], sm[:, 3, :]), "g11")
            AC.need("g8")
            AC.do(lambda e: e.activation(sm[:, 0, :], sm[:, 0, :], ACT.Ln), "la")
            AC.do(lambda e: e.activation(sm[:, 2, :], sm[:, 2, :], ACT.Ln), "g12")
            DV.need("g12", "g11")
            DV.do(lambda e: e.tensor_tensor(sm[:, 2, :], sm[:, 2, :], sm[:, 3, :], ALU.mult), "g13")
            DV.need("g13")
            DV.do(lambda e: e.tensor_tensor(sm[:, 2, :], sm[:, 2, :], sm[:, 4, :], ALU.add), "g14")
            DV.need("g14")
            DV.do(lambda e: e.tensor_tensor(sm[:, 2, :], sm[:, 2, :], sm[:, 1, :], ALU.mult), "g15")
            DV.need("g15")
            DV.do(lambda e: e.scalar_tensor_tensor(S(5), zb, 0.0, S(2), ALU.max, ALU.add), "beta")
            PE.need("la", "z", "upper", "lower", "ones")
            for i, m in enumerate((upper, ones, lower)):
                PE.do(lambda e, i=i, m=m: e.matmul(PS[2][:, 64 * i:64 * i + 64], m[:, :], sm[:, 0, :],
                                                  start=True, stop=True), "cum" if i == 2 else None)
            AC.need("cum")
            AC.do(lambda e: e.activation(sm[:, 6:9, :], PS[2][:, 0:192].rearrange("p (a n) -> p a n", a=3), ACT.Exp),
                  "cd")
            DV.need("cd", "beta")
            DV.do(lambda e: e.tensor_tensor(sm[:, 8, :], sm[:, 8, :], sm[:, 5, :], ALU.mult), "w2b")

        LA, BETA, CD, TD, W2B = 0, 5, 6, 7, 8

        def small4(i, T):
            return sm[:, i, 4 * T:4 * T + 4]

        def head_pe(T):
            b, c, s = T // 4, T % 4, T % 2
            PE.need("cd")
            for h in range(4):
                PE.need(("q", b, h), ("k", b, h))
            if T >= 1:
                PE.need(("ss", T - 1), ("attn", T - 1), ("dec", T - 1))
                if (T - 1) % 4 < 3:
                    PE.need(("kw", T - 1))
            for h in range(4):
                PE.do(lambda e, h=h: e.transpose(PS[2][:, 128 * h:128 * h + 128],
                                                 kT[:, b % 2, h, 128 * c:128 * c + 128], ident[:, :]),
                      ("kn", T) if h == 3 else None)
            for h in range(4):
                PE.do(lambda e, h=h: e.matmul(PS[3][:, 128 * h:128 * h + 128],
                                              kT[:, b % 2, h, 128 * c:128 * c + 128],
                                              qT[:, b % 2, h, 128 * c:128 * c + 128], start=True, stop=True),
                      ("S", T) if h == 3 else None)
            PL.need("la", "upper")
            if T >= 1:
                PL.need(("D", T - 1))
            for h in range(4):
                PL.do(lambda e, h=h: e.tensor_scalar(lau[:, 0, 128 * h:128 * h + 128], upper[:, :],
                                                     sm[:, LA, 4 * T + h:4 * T + h + 1], None, ALU.mult),
                      ("lau", T) if h == 3 else None)
            PE.need(("lau", T))
            PE.do(lambda e: e.matmul(PS[4][:, :], lower[:, :], lau[:, 0, :], start=True, stop=True), ("D", T))
            AC.need(("kn", T))
            if T >= 1:
                AC.need(("ss", T - 1))
            if T >= 2:
                AC.need(("rn", T - 2))
            for h in range(4):
                AC.do(lambda e, h=h: e.activation(junk[:, 128 * h:128 * h + 128], PS[2][:, 128 * h:128 * h + 128], ACT.Square,
                                                  accum_out=kn_s[:, s, 0, h:h + 1]), ("ss", T) if h == 3 else None)
            AC.need(("D", T))
            if T >= 2:
                AC.need(("attn", T - 2))
            AC.do(lambda e: e.activation(dec[:, s, :], PS[4][:, :], ACT.Exp), ("dec", T))
            PL.need(("ss", T), "w2b")
            if T >= 2 and (T - 2) % 4 < 3:
                PL.need(("kw", T - 2))
            PL.do(lambda e: e.tensor_scalar(kn_s[:, s, 1, :], kn_s[:, s, 0, :], 1e-24, None, ALU.max), ("mx", T))
            PL.need(("mx", T))
            PL.do(lambda e: e.tensor_tensor(kn_s[:, s, 2, :], kn_s[:, s, 1, :], half[:, :], ALU.pow), ("rn", T))
            PL.need(("rn", T))
            PL.do(lambda e: e.tensor_tensor(kn_s[:, s, 4, :], kn_s[:, s, 2, :], small4(W2B, T), ALU.mult), ("w2", T))
            PL.do(lambda e: e.tensor_tensor(kn_s[:, s, 3, :], kn_s[:, s, 2, :], small4(BETA, T), ALU.mult), ("w1", T))
            PL.need(("dec", T))
            PL.do(lambda e: e.affine_select(out=h4(dec[:, s, :]), in_=h4(dec[:, s, :]), compare_op=ALU.is_ge, fill=0.0,
                                            base=0, pattern=[[0, 4], [1, 128]], channel_multiplier=-1), ("mask", T))
            PL.need(("mask", T), ("w1", T))
            PL.do(lambda e: e.tensor_tensor(h4(dec[:, s, :]), h4(dec[:, s, :]),
                                            kn_s[:, s, 3, :].unsqueeze(2).broadcast_to([128, 4, 128]), ALU.mult),
                  ("decw", T))

        def head_dve(T):
            c, s = T % 4, T % 2
            if c < 3:
                DV.need(("kn", T), ("w2", T))
                if T >= 1:
                    DV.need(("dl", T - 1 if c else T - 2))
                DV.need(("ss", T))
                DV.do(lambda e: e.tensor_tensor(h4(kwb[:, 0, :]), h4(PS[2][:, :]),
                                                kn_s[:, s, 4, :].unsqueeze(2).broadcast_to([128, 4, 128]), ALU.mult),
                      ("kw", T))
            DV.need(("S", T), ("decw", T))
            if T >= 1:
                DV.need(("yl", T - 1))
            DV.do(lambda e: e.tensor_tensor(att[:, 0, :], PS[3][:, :], dec[:, s, :], ALU.mult), ("attn", T))

        def mid(T):
            b, c, s = T // 4, T % 4, T % 2
            PE.need(("v", b, c))
            if c < 3:
                PE.need(("kw", T))
                if T >= 4 or c > 0:
                    PE.need(("state", T - 1 if c else T - 2))
                for h in range(4):
                    PE.do(lambda e, h=h: e.matmul(PS[7][:, 128 * h:128 * h + 128], kwb[:, 0, 128 * h:128 * h + 128],
                                                  vv[:, b % 2, c, 128 * h:128 * h + 128], start=True, stop=True),
                          ("dl", T) if h == 3 else None)
            if c >= 1:
                PE.need(("state", T - 1))
                if T >= 2:
                    PE.need(("x1", T - 1))
                for h in range(4):
                    PE.do(lambda e, h=h: e.matmul(PS[6][:, 128 * h:128 * h + 128],
                                                  qT[:, b % 2, h, 128 * c:128 * c + 128],
                                                  st[:, (T - 1) % 2, 128 * h:128 * h + 128], start=True, stop=True),
                          ("yg", T) if h == 3 else None)
            PE.need(("attn", T))
            if T >= 1:
                PE.need(("yla", T - 1))
            for h in range(4):
                PE.do(lambda e, h=h: e.matmul(PS[5][:, 128 * h:128 * h + 128], att[:, 0, 128 * h:128 * h + 128],
                                              vv[:, b % 2, c, 128 * h:128 * h + 128], start=True, stop=True),
                      ("yl", T) if h == 3 else None)
            if c < 3:
                DV.need(("dl", T))
                if c == 0:
                    if T >= 4:
                        DV.need(("yg", T - 1))
                    DV.do(lambda e: e.tensor_copy(st[:, s, :], PS[7][:, :]), ("state", T))
                else:
                    DV.need(("state", T - 1))
                    if T >= 2 and c == 2:
                        DV.need(("yg", T - 1))
                    for h in range(4):
                        hs = slice(128 * h, 128 * h + 128)
                        DV.do(lambda e, h=h, hs=hs: e.scalar_tensor_tensor(
                            st[:, s, hs], st[:, 1 - s, hs], sm[:, TD, 4 * T + h:4 * T + h + 1], PS[7][:, hs],
                            ALU.mult, ALU.add), ("state", T) if h == 3 else None)
            DV.need(("yl", T))
            DV.do(lambda e: e.tensor_tensor(X1[:, T, :], X1[:, T, :], PS[5][:, :], ALU.add), ("yla", T))
            DV.need(("yla", T))
            if c >= 1:
                DV.need(("yg", T))
                for h in range(4):
                    hs = slice(128 * h, 128 * h + 128)
                    DV.do(lambda e, h=h, hs=hs: e.scalar_tensor_tensor(
                        X1[:, T, hs], PS[6][:, hs], sm[:, CD, 4 * T + h:4 * T + h + 1], X1[:, T, hs],
                        ALU.mult, ALU.add), ("x1", T) if h == 3 else None)
            else:
                marks[("x1", T)] = marks[("yla", T)]
            norm_stats("n2", T, X1[:, T, :], [("x1", T)])

        def tail_dve(T):
            war = [("n2", "t", T - 2)] if T >= 2 else [("n1", "t", NT - 1)]
            norm_apply("n2", T, X1[:, T, :], war)

        def tail(T):
            turn("n2", T, True)

        def upgate(i):
            g, b, j = i // 16, (i % 16) // 4, i % 4
            buf = WR[g % 2]
            pg, pu = PS[2 * (i % 2)], PS[2 * (i % 2) + 1]
            if i >= 2:
                PE.need(("inter", i - 2))
            elif i == 0:
                PE.need(*ring[-2:])
            else:
                PE.need(("kw", NT - 2), ("ss", NT - 1), ("attn", NT - 1))
            for T in range(4 * b, 4 * b + 4):
                PE.need(("n2", "hi", T), ("n2", "lo", T))
            for o, bank, name in ((0, pg, "gate"), (4, pu, "up")):
                for c in range(2):
                    for nib in range(2):
                        PE.need(("whi", 6 * g + o // 2 + c, nib), ("wlo", 6 * g + o // 2 + c, nib))
                n = 0
                for kt in range(4):
                    for xp, wp in XP:
                        PE.do(lambda e, bank=bank, o=o, kt=kt, xp=xp, wp=wp, n=n: e.matmul(
                            bank[:, :], buf[:, wp, o + kt, 128 * j:128 * j + 128], XT[:, xp, kt, 512 * b:512 * b + 512],
                            start=(n == 0), stop=(n == 11)), (name, i) if n == 11 else None)
                        n += 1

        GS = 1.0 / (XS * WS)

        def act_tile(i):
            s = i % 2
            pg, pu = PS[2 * s], PS[2 * s + 1]
            AC.need(("gate", i))
            if i >= 2:
                AC.need(("pp", i - 2))
            AC.do(lambda e: e.activation(sq[s], pg[:, :], ACT.Square, scale=CUB ** 0.5 * GS), ("sq", i))
            DV.need(("sq", i))
            if i >= 2:
                DV.need(("tanh", i - 2))
            DV.do(lambda e: e.scalar_tensor_tensor(pb[s], sq[s], 1.0, pg[:, :], ALU.add, ALU.mult), ("pp", i))
            AC.need(("pp", i))
            if i >= 2:
                AC.need(("wg", i - 2))
            AC.do(lambda e: e.activation(tnh[s], pb[s], ACT.Tanh, scale=GK * GS), ("tanh", i))
            DV.need(("tanh", i))
            DV.do(lambda e: e.scalar_tensor_tensor(wgb[s], tnh[s], 1.0, pg[:, :], ALU.add, ALU.mult), ("wg", i))
            DV.need(("wg", i), ("up", i))
            if i >= 2:
                DV.need(("ihi", i - 2))
            DV.do(lambda e: e.scalar_tensor_tensor(inf[s], wgb[s], 0.5 * GS * GS * IS, pu[:, :], ALU.mult, ALU.mult),
                  ("inter", i))
            q = i % 4
            AC.need(("inter", i))
            if i >= 4:
                AC.need(("dn", i - 4))
            AC.do(lambda e: e.copy(ihl[:, q, 0, :], inf[s]), ("ihi", i))
            DV.need(("ihi", i))
            DV.do(lambda e: e.tensor_tensor(ihl[:, q, 1, :], inf[s], ihl[:, q, 0, :], ALU.subtract), ("ilo", i))

        def down(i):
            g, b, j, q = i // 16, (i % 16) // 4, i % 4, i % 4
            buf = WR[g % 2]
            k = 6 * g + 4 + j // 2
            PE.need(("whi", k, j % 2), ("wlo", k, j % 2), ("ilo", i))
            if i == 0:
                PE.need(("dec", NT - 1), ("x1", NT - 1), ("state", NT - 2))
            for tt in range(4):
                if j == 0 and i >= 4:
                    PE.need(("ev", (i // 4 - 1) * 4 + tt))
                for n, (ip, wp) in enumerate(((0, 0), (0, 1), (1, 0))):
                    last = tt == 3 and n == 2
                    PE.do(lambda e, tt=tt, ip=ip, wp=wp, n=n: e.matmul(
                        PS[4 + tt][:, :], ihl[:, q, ip, 128 * tt:128 * tt + 128], buf[:, wp, 8 + j, :],
                        start=(j == 0 and n == 0), stop=(j == 3 and n == 2), skip_group_check=True),
                        ("dnt", i, tt) if (n == 2 and tt < 3 and j == 3) else (("dn", i) if last else None))

        def collect(i):
            g, b = i // 16, (i % 16) // 4
            for tt in range(4):
                T = 4 * b + tt
                DV.need(("dnt", i, tt) if tt < 3 else ("dn", i))
                DV.do(lambda e, tt=tt, T=T: e.scalar_tensor_tensor(
                    X1[:, T, :], PS[4 + tt][:, :], 1.0 / (WS * IS), X1[:, T, :], ALU.mult, ALU.add),
                    ("ev", (i // 4) * 4 + tt))

        for k in range(3):
            load_chunk(k)
        for T in range(NT):
            b = T // 4
            norm_stats("n1", T, X1[:, T, :], [("x", b)])
            if T >= 1:
                norm_apply("n1", T - 1, X1[:, T - 1, :], [("n1", "t", T - 3)] if T >= 3 else [])
                turn("n1", T - 1, False)
            if T % 4 == 3:
                wprep(T // 4)
            if T >= 2:
                logits(T - 2)
        norm_apply("n1", NT - 1, X1[:, NT - 1, :], [("n1", "t", NT - 3)])
        turn("n1", NT - 1, False)
        logits(NT - 2)
        logits(NT - 1)
        for kind, h in QKV[:4]:
            qkv(0, kind, h)
        gates()
        for kind, h in QKV[4:]:
            qkv(0, kind, h)

        nk = 0

        def dequant_some(n):
            nonlocal nk
            for _ in range(n):
                if nk < 48:
                    dq_bits(nk)
                    dq_mul(nk)
                    if nk + 3 < 48:
                        load_chunk(nk + 3)
                    nk += 1

        for T in range(NT):
            b, c = T // 4, T % 4
            fill = [(b + 1,) + QKV[3 * c + i] for i in range(3)] if b < 3 else []
            head_pe(T)
            for f in fill[:1]:
                qkv(*f)
            if T >= 1:
                tail_dve(T - 1)
                tail(T - 1)
            for f in fill[1:2]:
                qkv(*f)
            head_dve(T)
            if nk < 6:
                dequant_some(1)
            for f in fill[2:]:
                qkv(*f)
            if T == 11:
                marks["qkv_done"] = marks[("v", "mm", 3, 3)]
            mid(T)
        tail_dve(NT - 1)
        tail(NT - 1)

        for i in range(NI + 2):
            if i < NI:
                upgate(i)
            if i >= 2:
                down(i - 2)
            if i < NI:
                act_tile(i)
                if i % 16 in (0, 2, 4, 6, 8, 10):
                    dequant_some(1)
            if i >= 2 and (i - 2) % 4 == 3:
                collect(i - 2)
        ov = out.rearrange("(b i p) d -> b p i d", b=4, p=128)
        for b in range(4):
            SP.need(*[("ev", (NI // 4 - 4 + b) * 4 + tt) for tt in range(4)])
            SP.load(lambda e, b=b: e.dma_start(ov[b], X1[:, 4 * b:4 * b + 4, :]), ("out",), s_o, 64)
        SP.need(("out",))

        block = ctx.enter_context(nc.Block())

        @block.sync
        def _(eng):
            SP.emit(eng)

        @block.gpsimd
        def _(eng):
            PL.emit(eng)

        @block.scalar
        def _(eng):
            AC.emit(eng)

        @block.vector
        def _(eng):
            DV.emit(eng)

        @block.tensor
        def _(eng):
            PE.emit(eng)


def kernel(**inputs):
    import numpy as np
    import concourse.bacc as bacc
    from concourse.bass_utils import run_bass_kernel_spmd as run

    a = {k[3:]: np.asarray(v) for k, v in inputs.items()}
    n = np.arange(4096).reshape(16, 128, 2).transpose(0, 2, 1).reshape(-1)

    def gu_codes(w):
        return w[n].T.reshape(2, 128, 8, 512).transpose(2, 0, 1, 3)

    def gu_scales(w):
        return w[n].T.reshape(2, 8, 8, 512).transpose(2, 0, 1, 3)

    codes = np.concatenate([gu_codes(a["ffn_gate_W_packed"]), gu_codes(a["ffn_up_W_packed"]),
                            a["ffn_down_W_packed"].T.reshape(8, 2, 128, 512)], axis=1)
    scales = np.concatenate([gu_scales(a["ffn_gate_scales"]), gu_scales(a["ffn_up_scales"]),
                             a["ffn_down_scales"].T.reshape(8, 2, 8, 512)], axis=1)
    arrays = {
        "x": a["attn_x"].reshape(2048, 512),
        "wqkv": np.concatenate([a["attn_Wq"], a["attn_Wk"], a["attn_Wv"]], axis=1),
        "bqk": np.concatenate([a["attn_bq"].reshape(4, 128), a["attn_bk"].reshape(4, 128)]).T,
        "bv": a["attn_bv"].reshape(1, 512),
        "wab": np.concatenate([a["attn_Walpha"], a["attn_Wbeta"]], axis=1),
        "bab": np.concatenate([a["attn_balpha"], a["attn_bbeta"]]).reshape(1, 8),
        "codes": codes,
        "scales": scales,
    }
    arrays = {k: np.ascontiguousarray(v) for k, v in arrays.items()}
    nc = bacc.Bacc("TRN2", target_bir_lowering=False, num_devices=1)
    args = [nc.dram_tensor(k, v.shape, mybir.dt.from_np(v.dtype), kind="ExternalInput").ap() for k, v in arrays.items()]
    out = nc.dram_tensor("y", (2048, 512), F32, kind="ExternalOutput").ap()
    block_kernel(nc, *args, out)
    r = run(nc, [arrays], core_ids=[0])
    return r.results[0]["y"].reshape(4, 512, 512)
```

```python
from contextlib import ExitStack

import concourse.bass as bass
from concourse import mybir

F32 = mybir.dt.float32
F16 = mybir.dt.float16
I32 = mybir.dt.int32
ALU = mybir.AluOpType
ACT = mybir.ActivationFunctionType

NT = 16
NG = 8
NI = NG * 16

XS = 2.0 ** 11
QS = 2.0 ** 10
WS = 2.0 ** 10
IS = 2.0 ** -2
CODE = WS * 2.0 ** 14
GK = 0.7978845608028654
CUB = 0.044715


class Lane:

    def __init__(self, marks, sem):
        self.marks, self.sem, self.items, self.count = marks, sem, [], 0

    def do(self, fn, mark=None):
        if mark is not None:
            self.count += 1
            assert mark not in self.marks, mark
            self.marks[mark] = (self.sem, self.count)
        self.items.append((fn, mark))

    def load(self, fn, mark, sem, value):
        self.marks[mark] = (sem, value)
        self.items.append((fn, (sem,)))

    def need(self, *names):
        self.items.append((None, names))

    def emit(self, eng):
        seen = {}
        for fn, x in self.items:
            if fn is None:
                for name in x:
                    sem, value = self.marks[name]
                    if seen.get(sem.name, 0) < value:
                        eng.wait_ge(sem, value)
                        seen[sem.name] = value
                continue
            ins = fn(eng)
            if isinstance(x, tuple) and len(x) == 1 and not isinstance(x[0], str):
                ins.then_inc(x[0], 16)
            elif x is not None:
                ins.then_inc(self.sem, 1)


def block_kernel(nc, x, wqkv, bqk, bv, wab, bab, codes, scales, out):
    with ExitStack() as ctx:
        def sb(name, shape, dt):
            return ctx.enter_context(nc.sbuf_tensor(name, shape, dt))

        def sem(name):
            return ctx.enter_context(nc.semaphore(name))

        X1 = sb("X1", [128, NT, 512], F32)
        XT = sb("XT", [128, 2, 4, NT * 128], F16)
        WR0 = sb("WR0", [128, 2, 12, 512], F16)
        WR1 = sb("WR1", [128, 2, 12, 512], F16)
        REG = sb("REG", [128, 2, 2, 2048], F32)
        vv = sb("vv", [128, 4, 512], F32)
        raw = sb("raw", [128, 2, 512], I32)
        scl = sb("scl", [128, 2, 512], F32)
        tb = sb("tb", [128, 512], I32)
        wf = sb("wf", [128, 2, 512], F32)
        xh = sb("xh", [128, 2, 512], F32)
        dec = sb("dec", [128, 2, 512], F32)
        att = sb("att", [128, 512], F32)
        kwb = sb("kwb", [128, 512], F32)
        lau = sb("lau", [128, 512], F32)
        st = sb("st", [128, 2, 512], F32)
        fw = sb("fw", [128, 2, 512], F32)
        ihl_s = sb("ihl_s", [128, 4, 2, 512], F16)
        junk = sb("junk", [128, 512], mybir.dt.bfloat16)
        ident = sb("ident", [128, 128], F32)
        upper = sb("upper", [128, 128], F32)
        lower = sb("lower", [128, 128], F32)
        ones = sb("ones", [128, 128], F32)
        bvb = sb("bvb", [128, 512], F32)
        babb = sb("babb", [128, 8], F32)
        bqk_s = sb("bqk_s", [128, 8], F32)
        wab_f = sb("wab_f", [128, 4, 8], F32)
        wab_h = sb("wab_h", [128, 2, 4, 8], F16)
        z = sb("z", [128, NT, 8], F32)
        sm = sb("sm", [128, 9, 64], F32)
        bst = sb("bst", [128, 2, 6], F32)
        mv = sb("mv", [128, 2, 2], F32)
        rs = sb("rs", [128, 2, 2], F32)
        half = sb("half", [128, 4], F32)
        kn_s = sb("kn_s", [128, 2, 5, 4], F32)

        WR = [WR0, WR1]
        wq = WR1[:, :, :, :].rearrange("p a m n -> p (a m n)").rearrange("p (a k n) -> p a k n", a=2, k=4)
        qT = REG[:, 0, :, :].rearrange("p b (h t) -> p b h t", h=4)
        kT = REG[:, 1, :, :].rearrange("p b (h t) -> p b h t", h=4)
        flat = REG[:, :, :, :].rearrange("p a b n -> p (a b n)")
        wsrc = [flat[:, 1536 * k:1536 * k + 1536] for k in range(4)]
        ihl_r = flat[:, 0:2048].bitcast(F16).rearrange("p (s a t) -> p s a t", s=4, a=2)

        PS = [ctx.enter_context(nc.psum_tensor(f"ps{i}", [128, 512], F32)) for i in range(8)]

        s_pe, s_act, s_dve, s_pool = sem("s_pe"), sem("s_act"), sem("s_dve"), sem("s_pool")
        s_x = [sem(f"s_x{b}") for b in range(4)]
        s_w = [sem(f"s_w{k}") for k in range(4)]
        s_c = sem("s_c")
        s_d = [sem(f"s_d{k}") for k in range(2)]
        s_o = sem("s_o")

        marks = {}
        PE, AC, DV, PL = (Lane(marks, s) for s in (s_pe, s_act, s_dve, s_pool))
        SP = Lane(marks, None)

        def h4(ap):
            return ap.rearrange("p (h t) -> p h t", h=4)

        xv = x.rearrange("(b i p) d -> b p i d", b=4, p=128)
        wv = wqkv.rearrange("(k p) n -> k p n", p=128)

        def load_x(b):
            SP.load(lambda e: e.dma_start(X1[:, 4 * b:4 * b + 4, :], xv[b]), ("x", b), s_x[b], 16)

        def load_w(k):
            SP.load(lambda e: e.dma_start(wsrc[k], wv[k]), ("w", k), s_w[k], 16)

        load_x(0)
        for f in (lambda e: e.dma_start(wab_f[:, :, :], wab.rearrange("(k p) n -> p k n", p=128)),
                  lambda e: e.dma_start(bqk_s[:, :], bqk),
                  lambda e: e.dma_start(bvb[:, :], bv.broadcast_to([128, 512])),
                  lambda e: e.dma_start(babb[:, :], bab.broadcast_to([128, 8]))):
            SP.load(f, ("consts",), s_c, 64)
        for k in range(4):
            load_w(k)
        for b in range(1, 4):
            load_x(b)

        def load_chunk(k):
            s = k % 2
            if k >= 2:
                SP.need(("wf", k - 2, 1))
            SP.load(lambda e: e.dma_start(raw[:, s, :], codes[k // 6, k % 6]), ("raw", k), s_d[s], 32 * (k // 2 + 1))
            src = scales[k // 6, k % 6]
            rep = bass.AP(src.tensor, src.offset, [[512, 8], [0, 16], [1, 512]])
            SP.load(lambda e: e.dma_start(scl[:, s, :], rep), ("scl", k), s_d[s], 32 * (k // 2 + 1))

        PL.do(lambda e: e.memset(ident[:, :], 0.0), "z0")
        PL.do(lambda e: e.memset(ones[:, :], 1.0), "ones")
        PL.do(lambda e: e.memset(half[:, :], -0.5), "half")
        PL.need("half")
        PL.do(lambda e: e.affine_select(out=ident[:, :], in_=ident[:, :], compare_op=ALU.not_equal, fill=1.0,
                                        base=0, pattern=[[-1, 128]], channel_multiplier=1), "ident")
        PL.do(lambda e: e.affine_select(out=upper[:, :], in_=ones[:, :], compare_op=ALU.is_ge, fill=0.0,
                                        base=0, pattern=[[1, 128]], channel_multiplier=-1), "upper")
        PL.do(lambda e: e.affine_select(out=lower[:, :], in_=ones[:, :], compare_op=ALU.is_gt, fill=0.0,
                                        base=0, pattern=[[-1, 128]], channel_multiplier=1), "lower")

        ring = [0, 1, 5, 6, 7]
        freed = {bank: [] for bank in range(8)}
        turn_of = [0]

        def take(*released_by):
            bank = ring[turn_of[0] % len(ring)]
            turn_of[0] += 1
            PE.need(*freed[bank])
            freed[bank] = released_by
            return PS[bank]

        def norm_stats(tag, T, xt, pre):
            s = T % 2
            DV.need(*pre)
            DV.do(lambda e: e.bn_stats(bst[:, s, :], xt), (tag, "bs", T))
            DV.need((tag, "bs", T))
            DV.do(lambda e: e.bn_aggr(mv[:, s, :], bst[:, s, :]), (tag, "mv", T))
            PL.need((tag, "mv", T))
            PL.do(lambda e: e.tensor_scalar(rs[:, s, 0:1], mv[:, s, 1:2], 1e-5, XS ** -2, ALU.add, ALU.mult),
                  (tag, "ve", T))
            PL.need((tag, "ve", T))
            PL.do(lambda e: e.tensor_tensor(rs[:, s, 1:2], rs[:, s, 0:1], half[:, 0:1], ALU.pow), (tag, "rs", T))

        def norm_apply(tag, T, xt, war):
            s = T % 2
            DV.need((tag, "rs", T), *war)
            DV.do(lambda e: e.tensor_scalar(xh[:, s, :], xt, mv[:, s, 0:1], rs[:, s, 1:2], ALU.subtract, ALU.mult),
                  (tag, "xh", T))

        def turn(tag, T, strided):
            s = T % 2
            PE.need((tag, "xh", T))
            if tag == "n1" and T == 0:
                PE.need("ident")
            bank = take((tag, "lo", T))
            for kt in range(4):
                if strided:
                    src = xh[:, s, 256 * (kt // 2) + kt % 2:256 * (kt // 2) + 256:2]
                else:
                    src = xh[:, s, 128 * kt:128 * kt + 128]
                PE.do(lambda e, kt=kt, src=src: e.transpose(bank[:, 128 * kt:128 * kt + 128], src, ident[:, :]),
                      (tag, "t", T) if kt == 3 else None)
            hi = XT[:, 0, :, 128 * T:128 * T + 128]
            lo = XT[:, 1, :, 128 * T:128 * T + 128]
            AC.need((tag, "t", T))
            AC.do(lambda e: e.copy(hi, h4(bank[:, :])), (tag, "hi", T))

            def low():
                DV.need((tag, "hi", T))
                DV.do(lambda e: e.tensor_tensor(lo, h4(bank[:, :]), hi, ALU.subtract), (tag, "lo", T))
            return low

        XP = [(0, 0), (1, 0), (0, 1)]

        def logits(T):
            PE.need(("n1", "hi", T), ("n1", "lo", T), "wab")
            n = 0
            for kt in range(4):
                for xp, wp in XP:
                    PE.do(lambda e, kt=kt, xp=xp, wp=wp, n=n: e.matmul(
                        PS[4][:, 8 * T:8 * T + 8], XT[:, xp, kt, 128 * T:128 * T + 128], wab_h[:, wp, kt, :],
                        start=(n == 0), stop=(n == 11)), ("lg", T) if n == 11 else None)
                    n += 1

        DV.need(("consts",))
        AC.need(("consts",))
        AC.do(lambda e: e.mul(wab_h[:, 0, :, :], wab_f[:, :, :], QS), "wab_hi")
        DV.need("wab_hi")
        DV.do(lambda e: e.scalar_tensor_tensor(wab_h[:, 1, :, :], wab_f[:, :, :], QS, wab_h[:, 0, :, :],
                                               ALU.mult, ALU.subtract), "wab")

        def wprep(k):
            AC.need(("w", k))
            DV.need(("w", k))
            for j in range(3):
                src = wsrc[k][:, 512 * j:512 * j + 512]
                hi = wq[:, 0, k, 512 * j:512 * j + 512]
                lo = wq[:, 1, k, 512 * j:512 * j + 512]
                AC.do(lambda e, hi=hi, src=src: e.mul(hi, src, QS), ("wqh", k, j))
                DV.need(("wqh", k, j))
                DV.do(lambda e, hi=hi, lo=lo, src=src: e.scalar_tensor_tensor(lo, src, QS, hi, ALU.mult, ALU.subtract),
                      ("wql", k, j))

        def dq_bits(k):
            s = k % 2
            DV.need(("raw", k), ("scl", k))
            DV.do(lambda e: e.scalar_tensor_tensor(raw[:, s, :], raw[:, s, :], 12, raw[:, s, :],
                                                   ALU.logical_shift_left, ALU.bitwise_or), ("dt", k))
            DV.need(("dt", k))
            DV.do(lambda e: e.tensor_scalar(tb[:, :], raw[:, s, :], 9, 0x0E000E00, ALU.logical_shift_left,
                                            ALU.bitwise_and), ("du", k))
            DV.do(lambda e: e.tensor_scalar(raw[:, s, :], raw[:, s, :], 12, -0x7FFF8000, ALU.logical_shift_left,
                                            ALU.bitwise_and), ("dv", k))
            DV.need(("dv", k))
            DV.do(lambda e: e.tensor_tensor(tb[:, :], tb[:, :], raw[:, s, :], ALU.bitwise_or), ("dw", k))

        u16 = tb[:, :].bitcast(F16)

        def dq_mul(k):
            s, g, c = k % 2, k // 6, k % 6
            DV.need(("dw", k))
            for nib in range(2):
                if k >= 1:
                    DV.need(("wlo", k - 1, nib))
                DV.do(lambda e, nib=nib: e.scalar_tensor_tensor(wf[:, nib, :], u16[:, nib::2], CODE, scl[:, s, :],
                                                                ALU.mult, ALU.mult), ("wf", k, nib))
                buf, m = WR[g % 2], 2 * c + nib
                AC.need(("wf", k, nib))
                if g == 1:
                    AC.need(("v", "mm", 3, 3))
                if g >= 2:
                    AC.need(("dn", 4 * (g - 1) - 1, 3))
                AC.do(lambda e, nib=nib, buf=buf, m=m: e.copy(buf[:, 0, m, :], wf[:, nib, :]), ("whi", k, nib))
                PL.need(("whi", k, nib))
                PL.do(lambda e, nib=nib, buf=buf, m=m: e.tensor_tensor(buf[:, 1, m, :], wf[:, nib, :], buf[:, 0, m, :],
                                                                      ALU.subtract), ("wlo", k, nib))

        def qkv(b, kind, h):
            for T in range(4 * b, 4 * b + 4):
                PE.need(("n1", "hi", T), ("n1", "lo", T))
            for k in range(4):
                for j in range(3):
                    PE.need(("wqh", k, j), ("wql", k, j))
            bank = take((kind, b, h))
            n = 0
            for kt in range(4):
                for xp, wp in XP:
                    xs = XT[:, xp, kt, 512 * b:512 * b + 512]
                    if kind == "v":
                        lhs, rhs = xs[:, 128 * h:128 * h + 128], wq[:, wp, kt, 1024:1536]
                    else:
                        o = (0 if kind == "q" else 512) + 128 * h
                        lhs, rhs = wq[:, wp, kt, o:o + 128], xs
                    PE.do(lambda e, lhs=lhs, rhs=rhs, n=n: e.matmul(bank[:, :], lhs, rhs, start=(n == 0), stop=(n == 11)),
                          (kind, "mm", b, h) if n == 11 else None)
                    n += 1
            f = 1.0 / (XS * QS)
            if kind == "v":
                DV.need((kind, "mm", b, h))
                if b >= 1:
                    DV.need(("yl", 4 * b + h - 4))
                DV.do(lambda e: e.scalar_tensor_tensor(vv[:, h, :], bank[:, :], f, bvb[:, :], ALU.mult, ALU.add),
                      (kind, b, h))
            elif kind == "q":
                AC.need((kind, "mm", b, h))
                AC.do(lambda e: e.activation(qT[:, b % 2, h, :], bank[:, :], ACT.Identity, bias=bqk_s[:, h:h + 1],
                                             scale=f), (kind, b, h))
            else:
                DV.need((kind, "mm", b, h))
                DV.do(lambda e: e.tensor_scalar(kT[:, b % 2, h, :], bank[:, :], f, bqk_s[:, 4 + h:5 + h],
                                                ALU.mult, ALU.add), (kind, b, h))

        KQ = [(k, h) for h in range(4) for k in "kq"]

        def gates():
            zl = PS[4][:, 0:128].rearrange("p (t g) -> p t g", g=8)
            DV.need(("lg", NT - 1))
            DV.do(lambda e: e.scalar_tensor_tensor(
                z[:, :, :], zl, 1.0 / (XS * QS), babb[:, :].unsqueeze(1).broadcast_to([128, NT, 8]),
                ALU.mult, ALU.add), "z")
            za, zb = z[:, :, 0:4], z[:, :, 4:8]

            def S(i):
                return sm[:, i, :].rearrange("p (t h) -> p t h", h=4)

            DV.need("z")
            DV.do(lambda e: e.tensor_scalar(S(0), za, -1.0, 80.0, ALU.mult, ALU.min), "g0")
            DV.do(lambda e: e.scalar_tensor_tensor(S(1), zb, -1.0, zb, ALU.mult, ALU.min), "g1")
            AC.need("g1")
            AC.do(lambda e: e.activation(sm[:, 0, :], sm[:, 0, :], ACT.Exp), "g2")
            AC.do(lambda e: e.activation(sm[:, 1, :], sm[:, 1, :], ACT.Exp), "g3")
            DV.need("g3")
            DV.do(lambda e: e.tensor_scalar(sm[:, 0, :], sm[:, 0, :], 1.0, None, ALU.add), "g4")
            DV.do(lambda e: e.tensor_scalar(sm[:, 2, :], sm[:, 1, :], 1.0, None, ALU.add), "g5")
            DV.need("g5")
            DV.do(lambda e: e.reciprocal(sm[:, 0, :], sm[:, 0, :]), "g6")
            DV.do(lambda e: e.tensor_scalar(sm[:, 3, :], sm[:, 2, :], -1.0, None, ALU.add), "g7")
            DV.need("g7")
            DV.do(lambda e: e.tensor_scalar(sm[:, 0, :], sm[:, 0, :], 1e-6, None, ALU.add), "g8")
            DV.do(lambda e: e.tensor_scalar(sm[:, 4, :], sm[:, 3, :], 0.0, None, ALU.is_equal), "g9")
            DV.do(lambda e: e.tensor_scalar(sm[:, 3, :], sm[:, 3, :], 1e-9, None, ALU.max), "g10")
            DV.need("g10")
            DV.do(lambda e: e.reciprocal(sm[:, 3, :], sm[:, 3, :]), "g11")
            AC.need("g8")
            AC.do(lambda e: e.activation(sm[:, 0, :], sm[:, 0, :], ACT.Ln), "la")
            AC.do(lambda e: e.activation(sm[:, 2, :], sm[:, 2, :], ACT.Ln), "g12")
            DV.need("g12", "g11")
            DV.do(lambda e: e.tensor_tensor(sm[:, 2, :], sm[:, 2, :], sm[:, 3, :], ALU.mult), "g13")
            DV.need("g13")
            DV.do(lambda e: e.tensor_tensor(sm[:, 2, :], sm[:, 2, :], sm[:, 4, :], ALU.add), "g14")
            DV.need("g14")
            DV.do(lambda e: e.tensor_tensor(sm[:, 2, :], sm[:, 2, :], sm[:, 1, :], ALU.mult), "g15")
            DV.need("g15")
            DV.do(lambda e: e.scalar_tensor_tensor(S(5), zb, 0.0, S(2), ALU.max, ALU.add), "beta")
            PE.need("la", "z", "upper", "lower", "ones")
            for i, m in enumerate((upper, ones, lower)):
                PE.do(lambda e, i=i, m=m: e.matmul(PS[4][:, 64 * i:64 * i + 64], m[:, :], sm[:, 0, :],
                                                  start=True, stop=True), "cum" if i == 2 else None)
            AC.need("cum")
            AC.do(lambda e: e.activation(sm[:, 6:9, :], PS[4][:, 0:192].rearrange("p (a n) -> p a n", a=3), ACT.Exp),
                  "cd")
            DV.need("cd", "beta")
            DV.do(lambda e: e.tensor_tensor(sm[:, 8, :], sm[:, 8, :], sm[:, 5, :], ALU.mult), "w2b")

        LA, BETA, CD, TD, W2B = 0, 5, 6, 7, 8

        def small4(i, T):
            return sm[:, i, 4 * T:4 * T + 4]

        def decay(T):
            s = T % 2
            bank = take(("dec", T))
            PE.need(("lau", T))
            PE.do(lambda e: e.matmul(bank[:, :], lower[:, :], lau[:, :], start=True, stop=True), ("D", T))
            AC.need(("D", T))
            if T >= 2:
                AC.need(("attn", T - 2))
            AC.do(lambda e: e.activation(dec[:, s, :], bank[:, :], ACT.Exp), ("dec", T))

        def decay_rows(T):
            PL.need("la", "upper")
            if T >= 1:
                PL.need(("D", T - 1))
            PL.do(lambda e: e.tensor_tensor(h4(lau[:, :]), upper[:, :].unsqueeze(1).broadcast_to([128, 4, 128]),
                                            small4(LA, T).unsqueeze(2).broadcast_to([128, 4, 128]), ALU.mult),
                  ("lau", T))

        def decay_mask(T):
            s = T % 2
            PL.need(("dec", T))
            PL.do(lambda e: e.affine_select(out=h4(dec[:, s, :]), in_=h4(dec[:, s, :]), compare_op=ALU.is_ge, fill=0.0,
                                            base=0, pattern=[[0, 4], [1, 128]], channel_multiplier=-1), ("mask", T))

        def head(T):
            b, c, s = T // 4, T % 4, T % 2
            for h in range(4):
                PE.need(("q", b, h), ("k", b, h))
            kn = take(*([("ss", T), ("kw", T)] if c < 3 else [("ss", T)]))
            for h in range(4):
                PE.do(lambda e, h=h: e.transpose(kn[:, 128 * h:128 * h + 128],
                                                 kT[:, b % 2, h, 128 * c:128 * c + 128], ident[:, :]),
                      ("kn", T) if h == 3 else None)
            if T >= 1:
                PE.need(("attn", T - 1))
            else:
                PE.need("cd")
            for h in range(4):
                PE.do(lambda e, h=h: e.matmul(PS[4][:, 128 * h:128 * h + 128],
                                              kT[:, b % 2, h, 128 * c:128 * c + 128],
                                              qT[:, b % 2, h, 128 * c:128 * c + 128], start=True, stop=True),
                      ("S", T) if h == 3 else None)
            AC.need(("kn", T))
            if T >= 1:
                AC.need(("ss", T - 1))
            if T >= 2:
                AC.need(("rn", T - 2))
            for h in range(4):
                AC.do(lambda e, h=h: e.activation(junk[:, 128 * h:128 * h + 128], kn[:, 128 * h:128 * h + 128], ACT.Square,
                                                  accum_out=kn_s[:, s, 0, h:h + 1]), ("ss", T) if h == 3 else None)
            PL.need(("ss", T), "w2b")
            if T >= 2 and (T - 2) % 4 < 3:
                PL.need(("kw", T - 2))
            PL.do(lambda e: e.tensor_scalar(kn_s[:, s, 1, :], kn_s[:, s, 0, :], 1e-24, None, ALU.max), ("mx", T))
            PL.need(("mx", T))
            PL.do(lambda e: e.tensor_tensor(kn_s[:, s, 2, :], kn_s[:, s, 1, :], half[:, :], ALU.pow), ("rn", T))
            PL.need(("rn", T))
            PL.do(lambda e: e.tensor_tensor(kn_s[:, s, 4, :], kn_s[:, s, 2, :], small4(W2B, T), ALU.mult), ("w2", T))
            PL.do(lambda e: e.tensor_tensor(kn_s[:, s, 3, :], kn_s[:, s, 2, :], small4(BETA, T), ALU.mult), ("w1", T))
            PL.need(("mask", T), ("w1", T))
            PL.do(lambda e: e.tensor_tensor(h4(dec[:, s, :]), h4(dec[:, s, :]),
                                            kn_s[:, s, 3, :].unsqueeze(2).broadcast_to([128, 4, 128]), ALU.mult),
                  ("decw", T))
            return kn

        def weigh(T, kn):
            c, s = T % 4, T % 2
            if c < 3:
                DV.need(("kn", T), ("w2", T), ("ss", T))
                if T >= 1:
                    DV.need(("dl", T - 1 if c else T - 2))
                DV.do(lambda e: e.tensor_tensor(h4(kwb[:, :]), h4(kn[:, :]),
                                                kn_s[:, s, 4, :].unsqueeze(2).broadcast_to([128, 4, 128]), ALU.mult),
                      ("kw", T))
            DV.need(("S", T), ("decw", T))
            if T >= 1:
                DV.need(("yl", T - 1))
            DV.do(lambda e: e.tensor_tensor(att[:, :], PS[4][:, :], dec[:, s, :], ALU.mult), ("attn", T))

        def mid(T):
            b, c, s = T // 4, T % 4, T % 2
            PE.need(("v", b, c))
            if c < 3:
                dl = take(("state", T))
                PE.need(("kw", T))
                for h in range(4):
                    PE.do(lambda e, h=h: e.matmul(dl[:, 128 * h:128 * h + 128], kwb[:, 128 * h:128 * h + 128],
                                                  vv[:, c, 128 * h:128 * h + 128], start=True, stop=True),
                          ("dl", T) if h == 3 else None)
            yl = take(("yla", T))
            PE.need(("attn", T))
            for h in range(4):
                PE.do(lambda e, h=h: e.matmul(yl[:, 128 * h:128 * h + 128], att[:, 128 * h:128 * h + 128],
                                              vv[:, c, 128 * h:128 * h + 128], start=True, stop=True),
                      ("yl", T) if h == 3 else None)
            if c >= 1:
                yg = take(("x1", T))
                PE.need(("state", T - 1))
                for h in range(4):
                    PE.do(lambda e, h=h: e.matmul(yg[:, 128 * h:128 * h + 128],
                                                  qT[:, b % 2, h, 128 * c:128 * c + 128],
                                                  st[:, (T - 1) % 2, 128 * h:128 * h + 128], start=True, stop=True),
                          ("yg", T) if h == 3 else None)
            if c < 3:
                DV.need(("dl", T))
                if c == 0:
                    if T >= 4:
                        DV.need(("yg", T - 1))
                    DV.do(lambda e: e.tensor_copy(st[:, s, :], dl[:, :]), ("state", T))
                else:
                    DV.need(("state", T - 1))
                    if T >= 2 and c == 2:
                        DV.need(("yg", T - 1))
                    for h in range(4):
                        hs = slice(128 * h, 128 * h + 128)
                        DV.do(lambda e, h=h, hs=hs: e.scalar_tensor_tensor(
                            st[:, s, hs], st[:, 1 - s, hs], sm[:, TD, 4 * T + h:4 * T + h + 1], dl[:, hs],
                            ALU.mult, ALU.add), ("state", T) if h == 3 else None)
            DV.need(("yl", T))
            DV.do(lambda e: e.tensor_tensor(X1[:, T, :], X1[:, T, :], yl[:, :], ALU.add), ("yla", T))
            DV.need(("yla", T))
            if c >= 1:
                DV.need(("yg", T))
                for h in range(4):
                    hs = slice(128 * h, 128 * h + 128)
                    DV.do(lambda e, h=h, hs=hs: e.scalar_tensor_tensor(
                        X1[:, T, hs], yg[:, hs], sm[:, CD, 4 * T + h:4 * T + h + 1], X1[:, T, hs],
                        ALU.mult, ALU.add), ("x1", T) if h == 3 else None)
            else:
                marks[("x1", T)] = marks[("yla", T)]
            norm_stats("n2", T, X1[:, T, :], [("x1", T)])

        def tail_norm(T):
            war = [("n2", "t", T - 2)] if T >= 2 else [("n1", "t", NT - 2 + T)]
            norm_apply("n2", T, X1[:, T, :], war)

        def tail_turn(T):
            return turn("n2", T, True)

        def pair(i):
            return (PS[2], PS[3]) if i < 12 or i % 2 else (PS[4], PS[5])

        def upgate(i):
            g, b, j = i // 16, (i % 16) // 4, i % 4
            buf = WR[g % 2]
            pg, pu = pair(i)
            if i == 12:
                PE.need(("attn", NT - 1), *freed[5])
            elif i == 13:
                PE.need(("inter", 11))
            elif i >= 12:
                PE.need(("inter", i - 2))
            elif i >= 1:
                PE.need(("inter", i - 1))
            for T in range(4 * b, 4 * b + 4):
                PE.need(("n2", "hi", T), ("n2", "lo", T))
            for o, bank, name in ((0, pg, "gate"), (4, pu, "up")):
                for c in range(2):
                    for nib in range(2):
                        PE.need(("whi", 6 * g + o // 2 + c, nib), ("wlo", 6 * g + o // 2 + c, nib))
                n = 0
                for kt in range(4):
                    for xp, wp in XP:
                        PE.do(lambda e, bank=bank, o=o, kt=kt, xp=xp, wp=wp, n=n: e.matmul(
                            bank[:, :], buf[:, wp, o + kt, 128 * j:128 * j + 128], XT[:, xp, kt, 512 * b:512 * b + 512],
                            start=(n == 0), stop=(n == 11)), (name, i) if n == 11 else None)
                        n += 1

        GS = 1.0 / (XS * WS)

        def slot(i):
            n, j = i // 4, i % 4
            return ihl_r[:, j] if n >= 3 and n % 2 else ihl_s[:, j]

        def act_tile(i):
            s, n = i % 2, i // 4
            pg, pu = pair(i)
            w = fw[:, s, :]
            ih = slot(i)
            AC.need(("gate", i))
            if i >= 2:
                AC.need(("ilo", i - 2))
            AC.do(lambda e: e.activation(w, pg[:, :], ACT.Square, scale=CUB ** 0.5 * GS), ("sq", i))
            DV.need(("sq", i))
            DV.do(lambda e: e.scalar_tensor_tensor(w, w, 1.0, pg[:, :], ALU.add, ALU.mult), ("pp", i))
            AC.need(("pp", i))
            AC.do(lambda e: e.activation(w, w, ACT.Tanh, scale=GK * GS), ("tanh", i))
            DV.need(("tanh", i))
            DV.do(lambda e: e.scalar_tensor_tensor(w, w, 1.0, pg[:, :], ALU.add, ALU.mult), ("wg", i))
            DV.need(("wg", i), ("up", i))
            DV.do(lambda e: e.scalar_tensor_tensor(w, w, 0.5 * GS * GS * IS, pu[:, :], ALU.mult, ALU.mult),
                  ("inter", i))
            AC.need(("inter", i))
            before = n - 1 if n < 3 else (2 if n == 4 else (n - 2 if n > 4 else -1))
            if before >= 0:
                AC.need(("dn", before, 3))
            AC.do(lambda e: e.copy(ih[:, 0, :], w), ("ihi", i))
            DV.need(("ihi", i))
            DV.do(lambda e: e.tensor_tensor(ih[:, 1, :], w, ih[:, 0, :], ALU.subtract), ("ilo", i))

        def down(n, tt):
            g, b = n // 4, n % 4
            T = 4 * b + tt
            buf = WR[g % 2]
            bank = take(("ev", n, tt))
            m = 0
            for j in range(4):
                k = 6 * g + 4 + j // 2
                ih = slot(4 * n + j)
                PE.need(("whi", k, j % 2), ("wlo", k, j % 2), ("ilo", 4 * n + j))
                for ip, wp in ((0, 0), (0, 1), (1, 0)):
                    PE.do(lambda e, j=j, ih=ih, ip=ip, wp=wp, m=m: e.matmul(
                        bank[:, :], ih[:, ip, 128 * tt:128 * tt + 128], buf[:, wp, 8 + j, :],
                        start=(m == 0), stop=(m == 11)), ("dn", n, tt) if m == 11 else None)
                    m += 1

            def gather():
                DV.need(("dn", n, tt))
                DV.do(lambda e: e.scalar_tensor_tensor(
                    X1[:, T, :], bank[:, :], 1.0 / (WS * IS), X1[:, T, :], ALU.mult, ALU.add), ("ev", n, tt))
            return gather

        nk = 0

        def dequant(limit):
            nonlocal nk
            if nk < min(limit, 48):
                dq_bits(nk)
                dq_mul(nk)
                if nk + 2 < 48:
                    load_chunk(nk + 2)
                nk += 1

        for k in range(2):
            load_chunk(k)
        lows = {}
        items = [(0,) + it for it in KQ]
        for T in range(NT + 2):
            if T < NT:
                norm_stats("n1", T, X1[:, T, :], [("x", T // 4)])
            if 1 <= T <= NT:
                norm_apply("n1", T - 1, X1[:, T - 1, :], [("n1", "t", T - 3)] if T >= 3 else [])
                lows[T - 1] = turn("n1", T - 1, False)
            if T >= 2:
                lows[T - 2]()
            if 2 <= T < 6:
                wprep(T - 2)
            if T >= 2:
                logits(T - 2)
            if T >= 7 and items:
                qkv(*items.pop(0))
        while items:
            qkv(*items.pop(0))
        gates()
        nxt = [(1,) + it for it in KQ]
        dequant(6)
        for _ in range(4):
            qkv(*nxt.pop(0))
        dequant(6)
        for h in range(3):
            qkv(0, "v", h)
        decay_rows(0)
        decay(0)
        decay_mask(0)
        decay_rows(1)

        for T in range(NT):
            b, c = T // 4, T % 4
            i = T - 4
            fill = []
            if b == 0:
                fill.append(nxt.pop(0))
            elif b < 3:
                fill += [(b + 1,) + KQ[2 * c], (b + 1,) + KQ[2 * c + 1]]
            if T + 3 < NT:
                fill.append(((T + 3) // 4, "v", (T + 3) % 4))
            gathers = []
            if T >= 1:
                tail_norm(T - 1)
            kn = head(T)
            if T + 1 < NT:
                decay(T + 1)
                decay_mask(T + 1)
            if T + 2 < NT:
                decay_rows(T + 2)
            for f in fill[:1]:
                qkv(*f)
            if i >= 0 and i % 4 == 0 and i > 0:
                gathers = [down(i // 4 - 1, tt) for tt in range(4)]
            low = tail_turn(T - 1) if T >= 1 else None
            weigh(T, kn)
            if low:
                low()
            for f in gathers:
                f()
            for f in fill[1:]:
                qkv(*f)
            if i >= 0:
                upgate(i)
                act_tile(i)
            if b == 0:
                dequant(6)
            if T >= 13:
                dequant(12)
            mid(T)
        tail_norm(NT - 1)
        g0 = [down(2, tt) for tt in range(2)]
        low = tail_turn(NT - 1)
        g0 += [down(2, tt) for tt in range(2, 4)]
        low()
        for f in g0:
            f()
        ring[:] = [0, 1, 6, 7]

        for i in range(12, NI + 4):
            n, j = i // 4, i % 4
            if i < NI:
                upgate(i)
            f = down(n - 1, j) if n >= 4 else None
            if i < NI:
                act_tile(i)
                if i < 16:
                    dequant(12)
                elif i % 16 >= 5 and i % 2:
                    dequant(6 * (i // 16 + 2))
            if f:
                f()
        ov = out.rearrange("(t p) d -> t p d", p=128)
        for T in range(NT):
            SP.need(("ev", NI // 4 - 4 + T // 4, T % 4))
            SP.load(lambda e, T=T: e.dma_start(ov[T], X1[:, T, :]), ("out",), s_o, 16 * NT)
        SP.need(("out",))

        block = ctx.enter_context(nc.Block())

        @block.sync
        def _(eng):
            SP.emit(eng)

        @block.gpsimd
        def _(eng):
            PL.emit(eng)

        @block.scalar
        def _(eng):
            AC.emit(eng)

        @block.vector
        def _(eng):
            DV.emit(eng)

        @block.tensor
        def _(eng):
            PE.emit(eng)


def kernel(**inputs):
    import numpy as np
    import concourse.bacc as bacc
    from concourse.bass_utils import run_bass_kernel_spmd as run

    a = {k[3:]: np.asarray(v) for k, v in inputs.items()}
    n = np.arange(4096).reshape(16, 128, 2).transpose(0, 2, 1).reshape(-1)

    def gu_codes(w):
        return w[n].T.reshape(2, 128, 8, 512).transpose(2, 0, 1, 3)

    def gu_scales(w):
        return w[n].T.reshape(2, 8, 8, 512).transpose(2, 0, 1, 3)

    codes = np.concatenate([gu_codes(a["ffn_gate_W_packed"]), gu_codes(a["ffn_up_W_packed"]),
                            a["ffn_down_W_packed"].T.reshape(8, 2, 128, 512)], axis=1)
    scales = np.concatenate([gu_scales(a["ffn_gate_scales"]), gu_scales(a["ffn_up_scales"]),
                             a["ffn_down_scales"].T.reshape(8, 2, 8, 512)], axis=1)
    arrays = {
        "x": a["attn_x"].reshape(2048, 512),
        "wqkv": np.concatenate([a["attn_Wq"], a["attn_Wk"], a["attn_Wv"]], axis=1),
        "bqk": np.concatenate([a["attn_bq"].reshape(4, 128), a["attn_bk"].reshape(4, 128)]).T,
        "bv": a["attn_bv"].reshape(1, 512),
        "wab": np.concatenate([a["attn_Walpha"], a["attn_Wbeta"]], axis=1),
        "bab": np.concatenate([a["attn_balpha"], a["attn_bbeta"]]).reshape(1, 8),
        "codes": codes,
        "scales": scales,
    }
    arrays = {k: np.ascontiguousarray(v) for k, v in arrays.items()}
    nc = bacc.Bacc("TRN2", target_bir_lowering=False, num_devices=1)
    args = [nc.dram_tensor(k, v.shape, mybir.dt.from_np(v.dtype), kind="ExternalInput").ap() for k, v in arrays.items()]
    out = nc.dram_tensor("y", (2048, 512), F32, kind="ExternalOutput").ap()
    block_kernel(nc, *args, out)
    r = run(nc, [arrays], core_ids=[0])
    return r.results[0]["y"].reshape(4, 512, 512)
```

```python
from contextlib import ExitStack

import concourse.bass as bass
from concourse import mybir

F32 = mybir.dt.float32
F16 = mybir.dt.float16
I32 = mybir.dt.int32
ALU = mybir.AluOpType
ACT = mybir.ActivationFunctionType

NT = 16
NG = 8
NI = NG * 16

XS = 2.0 ** 9
QS = 2.0 ** 10
WS = 2.0 ** 10
IS = 2.0 ** -2
LS = 2.0 ** 8
CODE = WS * 2.0 ** 14
GK = 0.7978845608028654
CUB = 0.044715


class Lane:

    def __init__(self, marks, sem):
        self.marks, self.sem, self.items, self.count = marks, sem, [], 0

    def do(self, fn, mark=None):
        if mark is not None:
            self.count += 1
            assert mark not in self.marks, mark
            self.marks[mark] = (self.sem, self.count)
        self.items.append((fn, mark))

    def load(self, fn, mark, sem, value):
        self.marks[mark] = (sem, value)
        self.items.append((fn, (sem,)))

    def need(self, *names):
        self.items.append((None, names))

    def emit(self, eng):
        seen = {}
        for fn, x in self.items:
            if fn is None:
                for name in x:
                    sem, value = self.marks[name]
                    if seen.get(sem.name, 0) < value:
                        eng.wait_ge(sem, value)
                        seen[sem.name] = value
                continue
            ins = fn(eng)
            if isinstance(x, tuple) and len(x) == 1 and not isinstance(x[0], str):
                ins.then_inc(x[0], 16)
            elif x is not None:
                ins.then_inc(self.sem, 1)


def block_kernel(nc, x, wqkv, bqk, bv, wab, bab, codes, scales, out):
    with ExitStack() as ctx:
        def sb(name, shape, dt):
            return ctx.enter_context(nc.sbuf_tensor(name, shape, dt))

        def sem(name):
            return ctx.enter_context(nc.semaphore(name))

        X1 = sb("X1", [128, NT, 512], F32)
        XT = sb("XT", [128, 2, 4, NT * 128], F16)
        WR0 = sb("WR0", [128, 2, 12, 512], F16)
        WR1 = sb("WR1", [128, 2, 12, 512], F16)
        REG = sb("REG", [128, 2, 2, 2048], F32)
        vv = sb("vv", [128, 4, 512], F32)
        raw = sb("raw", [128, 2, 512], I32)
        scl = sb("scl", [128, 2, 512], F32)
        tb = sb("tb", [128, 512], I32)
        wf = sb("wf", [128, 2, 512], F32)
        lau_t = sb("lau_t", [128, 64], F32)
        la_h = sb("la_h", [128, 2, 64], F16)
        lower_h = sb("lower_h", [128, 128], F16)
        fw = sb("fw", [128, 2, 512], F32)
        ihl_s = sb("ihl_s", [128, 4, 2, 512], F16)
        junk = sb("junk", [128, 512], mybir.dt.bfloat16)
        babb = sb("babb", [128, 8], F32)
        bqk_s = sb("bqk_s", [128, 8], F32)
        wab_f = sb("wab_f", [128, 4, 8], F32)
        wab_h = sb("wab_h", [128, 2, 4, 8], F16)
        z = sb("z", [128, NT, 8], F32)
        sm = sb("sm", [128, 9, 64], F32)
        bst = sb("bst", [128, 2, 6], F32)
        mv = sb("mv", [128, 2, 2], F32)
        rs = sb("rs", [128, 2, 2], F32)
        half = sb("half", [128, 4], F32)
        kn_s = sb("kn_s", [128, 2, 5, 4], F32)

        bigA = sb("bigA", [128, 3072], F32)
        bigB = sb("bigB", [128, 2048], F32)
        bigC = sb("bigC", [128, 1024], F32)

        def two(ap):
            return ap.rearrange("p (s n) -> p s n", s=2)

        st, xh = two(bigA[:, 0:1024]), two(bigA[:, 1024:2048])
        lau = bigA[:, 2048:3072].bitcast(F16).rearrange("p (s a n) -> p s a n", s=2, a=2)
        dec, att, kwb = two(bigB[:, 0:1024]), bigB[:, 1024:1536], bigB[:, 1536:2048]
        ident, upper, lower, ones = (bigC[:, 128 * j:128 * j + 128] for j in range(4))
        bvb = bigC[:, 512:1024]

        WRX = bigA[:, :].bitcast(F16).rearrange("p (g a s k n) -> p g a s k n", g=2, a=2, s=3, k=2)
        R = [two(bigB[:, 512 * j:512 * j + 512]) for j in range(4)]
        s5b, tS, ub = bigB[:, 0:256], bigB[:, 512:1024], two(bigB[:, 1024:2048])
        wf2 = two(bigC[:, :])
        TB = [REG[:, b % 2, b // 2, :].bitcast(F16).rearrange("p (a t k n) -> p a t k n", a=2, t=4, k=2)
              for b in range(4)]

        WR = [WR0, WR1]
        wq = WR1[:, :, :, :].rearrange("p a m n -> p (a m n)").rearrange("p (a k n) -> p a k n", a=2, k=4)
        qT = REG[:, 0, :, :].rearrange("p b (h t) -> p b h t", h=4)
        kT = REG[:, 1, :, :].rearrange("p b (h t) -> p b h t", h=4)
        flat = vv[:, :, :].rearrange("p a n -> p (a n)")
        stage = WR0[:, :, :, :].rearrange("p a m n -> p (a m n)").bitcast(F32)
        wsrc = [stage[:, 2048 * j:2048 * j + 2048].rearrange("p (k n) -> p k n", k=4) for j in range(3)]
        ihl_r = flat[:, 0:2048].bitcast(F16).rearrange("p (s a t) -> p s a t", s=4, a=2)

        PS = [ctx.enter_context(nc.psum_tensor(f"ps{i}", [128, 512], F32)) for i in range(8)]

        s_pe, s_act, s_dve, s_pool = sem("s_pe"), sem("s_act"), sem("s_dve"), sem("s_pool")
        s_x = [sem(f"s_x{b}") for b in range(7)]
        s_w = [sem(f"s_w{j}") for j in range(3)]
        s_c = sem("s_c")
        s_d = [sem(f"s_d{k}") for k in range(2)]
        s_o = sem("s_o")

        marks = {}
        PE, AC, DV, PL = (Lane(marks, s) for s in (s_pe, s_act, s_dve, s_pool))
        SP = Lane(marks, None)

        def h4(ap):
            return ap.rearrange("p (h t) -> p h t", h=4)

        xv = x.rearrange("(b i p) d -> b p i d", b=4, p=128)
        wv = wqkv.rearrange("(k p) n -> k p n", p=128)

        def load_x(b):
            SP.load(lambda e: e.dma_start(X1[:, 4 * b:4 * b + 4, :], xv[b]), ("x", b), s_x[b], 16)

        def load_w(j):
            SP.load(lambda e: e.dma_start(wsrc[j], wv[:, :, 512 * j:512 * j + 512].rearrange("k p n -> p k n")),
                    ("w", j), s_w[j], 16)

        for T in range(4):
            SP.load(lambda e, T=T: e.dma_start(X1[:, T, :], xv[0, :, T, :]), ("xt", T), s_x[(0, 4, 5, 6)[T]], 16)
        load_w(1)
        for f in (lambda e: e.dma_start(wab_f[:, :, :], wab.rearrange("(k p) n -> p k n", p=128)),
                  lambda e: e.dma_start(bqk_s[:, :], bqk),
                  lambda e: e.dma_start(bvb[:, :], bv.broadcast_to([128, 512])),
                  lambda e: e.dma_start(babb[:, :], bab.broadcast_to([128, 8]))):
            SP.load(f, ("consts",), s_c, 64)
        load_x(1)
        load_w(0)
        load_w(2)
        load_x(2)
        load_x(3)

        def load_chunk(k):
            s = k % 2
            if k >= 2:
                SP.need(("wf", k - 2, 1))
            SP.load(lambda e: e.dma_start(raw[:, s, :], codes[k // 6, k % 6]), ("raw", k), s_d[s], 32 * (k // 2 + 1))
            src = scales[k // 6, k % 6]
            rep = bass.AP(src.tensor, src.offset, [[512, 8], [0, 16], [1, 512]])
            SP.load(lambda e: e.dma_start(scl[:, s, :], rep), ("scl", k), s_d[s], 32 * (k // 2 + 1))

        PL.do(lambda e: e.memset(ident[:, :], 0.0), "z0")
        PL.do(lambda e: e.memset(ones[:, :], 1.0), "ones")
        PL.do(lambda e: e.memset(half[:, :], -0.5), "half")
        PL.need("half")
        PL.do(lambda e: e.affine_select(out=ident[:, :], in_=ident[:, :], compare_op=ALU.not_equal, fill=1.0,
                                        base=0, pattern=[[-1, 128]], channel_multiplier=1), "ident")
        PL.do(lambda e: e.affine_select(out=upper[:, :], in_=ones[:, :], compare_op=ALU.is_ge, fill=0.0,
                                        base=0, pattern=[[1, 128]], channel_multiplier=-1), "upper")
        PL.do(lambda e: e.affine_select(out=lower[:, :], in_=ones[:, :], compare_op=ALU.is_gt, fill=0.0,
                                        base=0, pattern=[[-1, 128]], channel_multiplier=1), "lower")
        PL.need("lower")
        PL.do(lambda e: e.tensor_scalar(lower_h[:, :], lower[:, :], 1.0, None, ALU.mult), "lower_h")

        ring = [0, 1, 5, 6, 7]
        freed = {bank: [] for bank in range(8)}
        turn_of = [0]

        def take(*released_by):
            bank = ring[turn_of[0] % len(ring)]
            turn_of[0] += 1
            PE.need(*freed[bank])
            freed[bank] = released_by
            return PS[bank]

        def norm_stats(tag, T, xt, pre):
            s = T % 2
            DV.need(*pre)
            DV.do(lambda e: e.bn_stats(bst[:, s, :], xt), (tag, "bs", T))
            DV.need((tag, "bs", T))
            DV.do(lambda e: e.bn_aggr(mv[:, s, :], bst[:, s, :]), (tag, "mv", T))

        def norm_scale(tag, T):
            s = T % 2
            PL.need((tag, "mv", T))
            PL.do(lambda e: e.tensor_scalar(rs[:, s, 0:1], mv[:, s, 1:2], 1e-5, XS ** -2, ALU.add, ALU.mult),
                  (tag, "ve", T))
            PL.need((tag, "ve", T))
            PL.do(lambda e: e.tensor_tensor(rs[:, s, 1:2], rs[:, s, 0:1], half[:, 0:1], ALU.pow), (tag, "rs", T))

        def norm_apply(tag, T, xt, war):
            s = T % 2
            DV.need((tag, "rs", T), *war)
            DV.do(lambda e: e.tensor_scalar(xh[:, s, :], xt, mv[:, s, 0:1], rs[:, s, 1:2], ALU.subtract, ALU.mult),
                  (tag, "xh", T))

        def turn(tag, T, strided):
            s = T % 2
            PE.need((tag, "xh", T))
            if tag == "n1" and T == 0:
                PE.need("ident")
            bank = take((tag, "lo", T))
            for kt in range(4):
                if strided:
                    src = xh[:, s, 256 * (kt // 2) + kt % 2:256 * (kt // 2) + 256:2]
                else:
                    src = xh[:, s, 128 * kt:128 * kt + 128]
                PE.do(lambda e, kt=kt, src=src: e.transpose(bank[:, 128 * kt:128 * kt + 128], src, ident[:, :]),
                      (tag, "t", T) if kt == 3 else None)
            hi = XT[:, 0, :, 128 * T:128 * T + 128]
            lo = XT[:, 1, :, 128 * T:128 * T + 128]
            AC.need((tag, "t", T))
            AC.do(lambda e: e.copy(hi, h4(bank[:, :])), (tag, "hi", T))

            def low():
                DV.need((tag, "hi", T))
                DV.do(lambda e: e.tensor_tensor(lo, h4(bank[:, :]), hi, ALU.subtract), (tag, "lo", T))
            return low

        XP = [(0, 0), (1, 0), (0, 1)]

        def logits(T):
            PE.need(("n1", "hi", T), ("n1", "lo", T), "wab")
            n = 0
            for kt in range(4):
                for xp, wp in XP:
                    PE.do(lambda e, kt=kt, xp=xp, wp=wp, n=n: e.matmul(
                        PS[4][:, 8 * T:8 * T + 8], XT[:, xp, kt, 128 * T:128 * T + 128], wab_h[:, wp, kt, :],
                        start=(n == 0), stop=(n == 11)), ("lg", T) if n == 11 else None)
                    n += 1

        def prep_ab():
            DV.need(("consts",))
            AC.need(("consts",))
            AC.do(lambda e: e.mul(wab_h[:, 0, :, :], wab_f[:, :, :], QS), "wab_hi")
            DV.need("wab_hi")
            DV.do(lambda e: e.scalar_tensor_tensor(wab_h[:, 1, :, :], wab_f[:, :, :], QS, wab_h[:, 0, :, :],
                                                   ALU.mult, ALU.subtract), "wab")

        def wprep(j):
            AC.need(("w", j))
            for k in range(4):
                src, hi = wsrc[j][:, k, :], wq[:, 0, k, 512 * j:512 * j + 512]
                AC.do(lambda e, hi=hi, src=src: e.mul(hi, src, QS), ("wqh", k, j))

            def low(ks=range(4)):
                DV.need(("w", j))
                for k in ks:
                    src, hi = wsrc[j][:, k, :], wq[:, 0, k, 512 * j:512 * j + 512]
                    lo = wq[:, 1, k, 512 * j:512 * j + 512]
                    DV.need(("wqh", k, j))
                    DV.do(lambda e, hi=hi, lo=lo, src=src: e.scalar_tensor_tensor(lo, src, QS, hi, ALU.mult,
                                                                                 ALU.subtract), ("wql", k, j))
            return low

        def dq_bits(k):
            s = k % 2
            DV.need(("raw", k), ("scl", k))
            DV.do(lambda e: e.scalar_tensor_tensor(raw[:, s, :], raw[:, s, :], 12, raw[:, s, :],
                                                   ALU.logical_shift_left, ALU.bitwise_or), ("dt", k))
            DV.need(("dt", k))
            DV.do(lambda e: e.tensor_scalar(tb[:, :], raw[:, s, :], 9, 0x0E000E00, ALU.logical_shift_left,
                                            ALU.bitwise_and), ("du", k))
            DV.do(lambda e: e.tensor_scalar(raw[:, s, :], raw[:, s, :], 12, -0x7FFF8000, ALU.logical_shift_left,
                                            ALU.bitwise_and), ("dv", k))
            DV.need(("dv", k))
            DV.do(lambda e: e.tensor_tensor(tb[:, :], tb[:, :], raw[:, s, :], ALU.bitwise_or), ("dw", k))

        u16 = tb[:, :].bitcast(F16)

        def dq_mul(k):
            s, g, c = k % 2, k // 6, k % 6
            DV.need(("dw", k))
            for nib in range(2):
                if k >= 1:
                    DV.need(("wlo", k - 1, nib))
                DV.do(lambda e, nib=nib: e.scalar_tensor_tensor(wf[:, nib, :], u16[:, nib::2], CODE, scl[:, s, :],
                                                                ALU.mult, ALU.mult), ("wf", k, nib))
                buf, m = WR[g % 2], 2 * c + nib
                AC.need(("wf", k, nib))
                if g == 0:
                    AC.need(*[("wql", kt, j) for kt in range(4) for j in range(3)])
                if g == 1:
                    AC.need(("v", "mm", 3, 3))
                if g >= 2:
                    AC.need(("dn", 4 * (g - 1) - 1, 3))
                AC.do(lambda e, nib=nib, buf=buf, m=m: e.copy(buf[:, 0, m, :], wf[:, nib, :]), ("whi", k, nib))
                PL.need(("whi", k, nib))
                PL.do(lambda e, nib=nib, buf=buf, m=m: e.tensor_tensor(buf[:, 1, m, :], wf[:, nib, :], buf[:, 0, m, :],
                                                                      ALU.subtract), ("wlo", k, nib))

        def tiles(ap, odd):
            return ap.rearrange("p k (u e n) -> p k u e n", u=2, e=2)[:, :, :, odd, :]

        def flat4(ap):
            return ap.rearrange("p (k u n) -> p k u n", k=2, u=2)

        def dq_up0(k):
            s, buf = k % 2, WR[k // 6 % 2]
            DV.need(("dw", k), ("wlo", k - 1, 0), ("wlo", k - 1, 1))
            for nib in range(2):
                DV.do(lambda e, nib=nib: e.scalar_tensor_tensor(wf[:, nib, :], u16[:, nib::2], CODE, scl[:, s, :],
                                                                ALU.mult, ALU.mult), ("wf", k, nib))
            src = tiles(wf[:, :, :], 0)
            hi, lo = (tiles(buf[:, a, 4:6, :], 0) for a in range(2))
            AC.need(("wf", k, 1), ("dn", 4 * (k // 6 - 1) - 1, 3))
            AC.do(lambda e: e.copy(hi, src), ("whi", k, 0))
            PL.need(("whi", k, 0))
            PL.do(lambda e: e.tensor_tensor(lo, src, hi, ALU.subtract), ("wlo", k, 0))
            marks[("whi", k, 1)], marks[("wlo", k, 1)] = marks[("whi", k, 0)], marks[("wlo", k, 0)]

        def dq_up1(k):
            s, buf = k % 2, WR[k // 6 % 2]
            DV.need(("dw", k), ("wlo", k - 1, 0))
            if k // 6 == 2:
                DV.need(("n2", "t", NT - 1))
            for nib in range(2):
                DV.do(lambda e, nib=nib: e.scalar_tensor_tensor(wf2[:, nib, :], u16[:, nib::2], CODE, scl[:, s, :],
                                                                ALU.mult, ALU.mult), ("wf", k, nib))
            for nib in range(2):
                AC.need(("wf", k, nib))
                AC.do(lambda e, nib=nib: e.copy(buf[:, 0, 6 + nib, :], wf2[:, nib, :]), ("whi", k, nib))
                PL.need(("whi", k, nib))
                PL.do(lambda e, nib=nib: e.tensor_tensor(buf[:, 1, 6 + nib, :], wf2[:, nib, :], buf[:, 0, 6 + nib, :],
                                                         ALU.subtract), ("wl1", k, nib))
            a11, a21, a12, a22 = tiles(wf[:, :, :], 0), tiles(wf[:, :, :], 1), tiles(wf2, 0), tiles(wf2, 1)
            PL.need(("tlo", 3, 3) if k == 15 else ("wlo", k - 6, 1))
            PL.do(lambda e: e.tensor_tensor(flat4(tS), a11, a21, ALU.subtract), ("S3", k))
            PL.need(("S3", k))
            PL.do(lambda e: e.tensor_tensor(a21, a21, a22, ALU.add), ("S1", k))
            PL.need(("S1", k))
            PL.do(lambda e: e.tensor_tensor(a11, a21, a11, ALU.subtract), ("S2", k))
            PL.need(("S2", k), ("wl1", k, 1))
            PL.do(lambda e: e.tensor_tensor(a12, a12, a11, ALU.subtract), ("S4", k))

        def dq_up2(k):
            g = k // 6 % 2
            a11, a21, a12 = tiles(wf[:, :, :], 0), tiles(wf[:, :, :], 1), tiles(wf2, 0)

            def wide(a, j):
                return WRX[:, g, a, j].rearrange("p k (u n) -> p k u n", u=2)

            parts = [(a21, [tiles(WR[g][:, a, 4:6, :], 1) for a in range(2)]), (a11, [wide(a, 0) for a in range(2)]),
                     (flat4(tS), [wide(a, 1) for a in range(2)]), (a12, [wide(a, 2) for a in range(2)])]
            AC.need(("S4", k))
            for j, (src, (hi, lo)) in enumerate(parts):
                AC.do(lambda e, src=src, hi=hi: e.copy(hi, src), ("shi", k, j))
                PL.need(("shi", k, j))
                PL.do(lambda e, src=src, hi=hi, lo=lo: e.tensor_tensor(lo, src, hi, ALU.subtract),
                      ("wlo", k, 1) if j == 3 else None)
            marks[("wlo", k, 0)] = marks[("wlo", k, 1)]

        def pair_sums(i):
            b, j = (i - 16) // 3, (i - 16) % 3
            quad = [(0, 0), (0, 256), (2, 0), (2, 256)]
            if j == 0:
                for T in range(4 * b, 4 * b + 4):
                    PL.need(("n2", "lo", T))
                PL.need(("yl", NT - 1), ("attn", NT - 1))
                if b:
                    PL.need(("tlo", b - 1, 3))
                for q, (k, o) in enumerate(quad):
                    hi, lo = (XT[:, a, k:k + 2, 512 * b + o:512 * b + o + 256] for a in range(2))
                    PL.do(lambda e, q=q, hi=hi, lo=lo: e.tensor_tensor(R[q], hi, lo, ALU.add), ("R", b, q))
            if j == 1:
                for name, out, x, y, before in (("T1", 0, 1, 0, ("R", b, 3)), ("T3", 1, 3, 1, ("T1", b)),
                                                ("T2", 3, 3, 0, ("T3", b)), ("T4", 2, 2, 3, ("T2", b))):
                    PL.need(before)
                    PL.do(lambda e, out=out, x=x, y=y: e.tensor_tensor(R[out], R[x], R[y], ALU.subtract), (name, b))
            if j == 2:
                AC.need(("T4", b), ("yg", NT - 1))
                for t, q in enumerate((0, 3, 1, 2)):
                    AC.do(lambda e, t=t, q=q: e.copy(TB[b][:, 0, t], R[q]), ("thi", b, t))
                    PL.need(("thi", b, t))
                    PL.do(lambda e, t=t, q=q: e.tensor_tensor(TB[b][:, 1, t], R[q], TB[b][:, 0, t], ALU.subtract),
                          ("tlo", b, t))

        def qkv(b, kind, h):
            for T in range(4 * b, 4 * b + 4):
                PE.need(("n1", "hi", T), ("n1", "lo", T))
            j = "qkv".index(kind)
            bank = take((kind, b, h))
            n = 0
            for kt in range(4):
                PE.need(("wqh", kt, j), ("wql", kt, j))
                for xp, wp in XP:
                    xs = XT[:, xp, kt, 512 * b:512 * b + 512]
                    if kind == "v":
                        lhs, rhs = xs[:, 128 * h:128 * h + 128], wq[:, wp, kt, 1024:1536]
                    else:
                        o = (0 if kind == "q" else 512) + 128 * h
                        lhs, rhs = wq[:, wp, kt, o:o + 128], xs
                    PE.do(lambda e, lhs=lhs, rhs=rhs, n=n: e.matmul(bank[:, :], lhs, rhs, start=(n == 0), stop=(n == 11)),
                          (kind, "mm", b, h) if n == 11 else None)
                    n += 1
            f = 1.0 / (XS * QS)

            def post():
                (AC if kind == "q" else DV).need(("consts",))
                if kind == "v":
                    DV.need((kind, "mm", b, h))
                    if b >= 1:
                        DV.need(("yl", 4 * b + h - 4))
                    DV.do(lambda e: e.scalar_tensor_tensor(vv[:, h, :], bank[:, :], f, bvb[:, :], ALU.mult, ALU.add),
                          (kind, b, h))
                elif kind == "q":
                    AC.need((kind, "mm", b, h))
                    AC.do(lambda e: e.activation(qT[:, b % 2, h, :], bank[:, :], ACT.Identity, bias=bqk_s[:, h:h + 1],
                                                 scale=f), (kind, b, h))
                else:
                    DV.need((kind, "mm", b, h))
                    DV.do(lambda e: e.tensor_scalar(kT[:, b % 2, h, :], bank[:, :], f, bqk_s[:, 4 + h:5 + h],
                                                    ALU.mult, ALU.add), (kind, b, h))
            return post

        KQ = [(k, h) for h in range(4) for k in "kq"]

        def gates():
            zl = PS[4][:, 0:128].rearrange("p (t g) -> p t g", g=8)
            DV.need(("lg", NT - 1))
            DV.do(lambda e: e.scalar_tensor_tensor(
                z[:, :, :], zl, 1.0 / (XS * QS), babb[:, :].unsqueeze(1).broadcast_to([128, NT, 8]),
                ALU.mult, ALU.add), "z")
            za, zb = z[:, :, 0:4], z[:, :, 4:8]

            def S(i):
                return sm[:, i, :].rearrange("p (t h) -> p t h", h=4)

            DV.need("z")
            DV.do(lambda e: e.tensor_scalar(S(0), za, -1.0, 80.0, ALU.mult, ALU.min), "g0")
            DV.do(lambda e: e.scalar_tensor_tensor(S(1), zb, -1.0, zb, ALU.mult, ALU.min), "g1")
            AC.need("g1")
            AC.do(lambda e: e.activation(sm[:, 0, :], sm[:, 0, :], ACT.Exp), "g2")
            AC.do(lambda e: e.activation(sm[:, 1, :], sm[:, 1, :], ACT.Exp), "g3")
            DV.need("g3")
            DV.do(lambda e: e.tensor_scalar(sm[:, 0, :], sm[:, 0, :], 1.0, None, ALU.add), "g4")
            DV.do(lambda e: e.tensor_scalar(sm[:, 2, :], sm[:, 1, :], 1.0, None, ALU.add), "g5")
            DV.need("g5")
            DV.do(lambda e: e.reciprocal(sm[:, 0, :], sm[:, 0, :]), "g6")
            DV.do(lambda e: e.tensor_scalar(sm[:, 3, :], sm[:, 2, :], -1.0, None, ALU.add), "g7")
            DV.need("g7")
            DV.do(lambda e: e.tensor_scalar(sm[:, 0, :], sm[:, 0, :], 1e-6, None, ALU.add), "g8")
            DV.do(lambda e: e.tensor_scalar(sm[:, 4, :], sm[:, 3, :], 0.0, None, ALU.is_equal), "g9")
            DV.do(lambda e: e.tensor_scalar(sm[:, 3, :], sm[:, 3, :], 1e-9, None, ALU.max), "g10")
            DV.need("g10")
            DV.do(lambda e: e.reciprocal(sm[:, 3, :], sm[:, 3, :]), "g11")
            AC.need("g8")
            AC.do(lambda e: e.activation(sm[:, 0, :], sm[:, 0, :], ACT.Ln), "la")
            AC.do(lambda e: e.activation(sm[:, 2, :], sm[:, 2, :], ACT.Ln), "g12")
            AC.need("la")
            AC.do(lambda e: e.mul(la_h[:, 0, :], sm[:, 0, :], LS), "lah")
            PL.need("lah")
            PL.do(lambda e: e.tensor_scalar(lau_t[:, :], sm[:, 0, :], LS, None, ALU.mult), "las")
            PL.need("las")
            PL.do(lambda e: e.tensor_tensor(la_h[:, 1, :], lau_t[:, :], la_h[:, 0, :], ALU.subtract), "lal")
            DV.need("g12", "g11")
            DV.do(lambda e: e.tensor_tensor(sm[:, 2, :], sm[:, 2, :], sm[:, 3, :], ALU.mult), "g13")
            DV.need("g13")
            DV.do(lambda e: e.tensor_tensor(sm[:, 2, :], sm[:, 2, :], sm[:, 4, :], ALU.add), "g14")
            DV.need("g14")
            DV.do(lambda e: e.tensor_tensor(sm[:, 2, :], sm[:, 2, :], sm[:, 1, :], ALU.mult), "g15")
            DV.need("g15")
            DV.do(lambda e: e.scalar_tensor_tensor(S(5), zb, 0.0, S(2), ALU.max, ALU.add), "beta")

        def gates_sum():
            PE.need("la", "z", "upper", "lower", "ones")
            for i, m in enumerate((upper, ones, lower)):
                PE.do(lambda e, i=i, m=m: e.matmul(PS[4][:, 64 * i:64 * i + 64], m[:, :], sm[:, 0, :],
                                                  start=True, stop=True), "cum" if i == 2 else None)
            AC.need("cum")
            AC.do(lambda e: e.activation(sm[:, 6:9, :], PS[4][:, 0:192].rearrange("p (a n) -> p a n", a=3), ACT.Exp),
                  "cd")
            DV.need("cd", "beta")
            DV.do(lambda e: e.tensor_tensor(sm[:, 8, :], sm[:, 8, :], sm[:, 5, :], ALU.mult), "w2b")

        LA, BETA, CD, TD, W2B = 0, 5, 6, 7, 8

        def small4(i, T):
            return sm[:, i, 4 * T:4 * T + 4]

        def decay(T):
            s = T % 2
            bank = take(("dec", T))
            PE.need("lower_h", ("lau", T))
            PE.do(lambda e: e.matmul(bank[:, :], lower_h[:, :], lau[:, s, 0, :], start=True, stop=False))
            PE.do(lambda e: e.matmul(bank[:, :], lower_h[:, :], lau[:, s, 1, :], start=False, stop=True), ("D", T))
            AC.need(("D", T))
            if T >= 2:
                AC.need(("attn", T - 2))
            AC.do(lambda e: e.activation(dec[:, s, :], bank[:, :], ACT.Exp, scale=1.0 / LS), ("dec", T))

        def decay_rows(T):
            PL.need("lal", "upper")
            if T >= 2:
                PL.need(("D", T - 2))
            for p in range(2):
                PL.do(lambda e, p=p: e.tensor_tensor(
                    h4(lau[:, T % 2, p, :]), upper[:, :].unsqueeze(1).broadcast_to([128, 4, 128]),
                    la_h[:, p, 4 * T:4 * T + 4].unsqueeze(2).broadcast_to([128, 4, 128]), ALU.mult),
                    ("lau", T) if p else None)

        def decay_mask(T):
            s = T % 2
            PL.need(("dec", T))
            PL.do(lambda e: e.affine_select(out=h4(dec[:, s, :]), in_=h4(dec[:, s, :]), compare_op=ALU.is_ge, fill=0.0,
                                            base=0, pattern=[[0, 4], [1, 128]], channel_multiplier=-1), ("mask", T))

        def head(T, early):
            b, c, s = T // 4, T % 4, T % 2
            for h in range(4):
                PE.need(("q", b, h), ("k", b, h))
            kn = take(*([("ss", T), ("kw", T)] if c < 3 else [("ss", T)]))
            for h in range(4):
                PE.do(lambda e, h=h: e.transpose(kn[:, 128 * h:128 * h + 128],
                                                 kT[:, b % 2, h, 128 * c:128 * c + 128], ident[:, :]),
                      ("kn", T) if h == 3 else None)
            if T >= 1:
                PE.need(("attn", T - 1))
            else:
                PE.need("cd")
            for h in range(4):
                PE.do(lambda e, h=h: e.matmul(PS[4][:, 128 * h:128 * h + 128],
                                              kT[:, b % 2, h, 128 * c:128 * c + 128],
                                              qT[:, b % 2, h, 128 * c:128 * c + 128], start=True, stop=True),
                      ("S", T) if h == 3 else None)
            AC.need(("kn", T))
            if T >= 1:
                AC.need(("ss", T - 1))
            if T >= 2:
                AC.need(("rn", T - 2))
            for h in range(4):
                AC.do(lambda e, h=h: e.activation(junk[:, 128 * h:128 * h + 128], kn[:, 128 * h:128 * h + 128], ACT.Square,
                                                  accum_out=kn_s[:, s, 0, h:h + 1]), ("ss", T) if h == 3 else None)
            PL.need(("ss", T), "w2b")
            if T >= 2 and (T - 2) % 4 < 3:
                PL.need(("kw", T - 2))
            PL.do(lambda e: e.tensor_scalar(kn_s[:, s, 1, :], kn_s[:, s, 0, :], 1e-24, None, ALU.max), ("mx", T))
            PL.need(("mx", T))
            PL.do(lambda e: e.tensor_tensor(kn_s[:, s, 2, :], kn_s[:, s, 1, :], half[:, :], ALU.pow), ("rn", T))
            PL.need(("rn", T))
            PL.do(lambda e: e.tensor_tensor(kn_s[:, s, 4, :], kn_s[:, s, 2, :], small4(W2B, T), ALU.mult), ("w2", T))
            PL.do(lambda e: e.tensor_tensor(kn_s[:, s, 3, :], kn_s[:, s, 2, :], small4(BETA, T), ALU.mult), ("w1", T))
            early()
            PL.need(("mask", T), ("w1", T))
            PL.do(lambda e: e.tensor_tensor(h4(dec[:, s, :]), h4(dec[:, s, :]),
                                            kn_s[:, s, 3, :].unsqueeze(2).broadcast_to([128, 4, 128]), ALU.mult),
                  ("decw", T))
            return kn

        def weigh_k(T, kn):
            c, s = T % 4, T % 2
            if c < 3:
                DV.need(("kn", T), ("w2", T), ("ss", T))
                if T >= 1:
                    DV.need(("dl", T - 1 if c else T - 2))
                DV.do(lambda e: e.tensor_tensor(h4(kwb[:, :]), h4(kn[:, :]),
                                                kn_s[:, s, 4, :].unsqueeze(2).broadcast_to([128, 4, 128]), ALU.mult),
                      ("kw", T))

        def weigh_s(T):
            s = T % 2
            DV.need(("S", T), ("decw", T))
            if T >= 1:
                DV.need(("yl", T - 1))
            DV.do(lambda e: e.tensor_tensor(att[:, :], PS[4][:, :], dec[:, s, :], ALU.mult), ("attn", T))

        def mid(T):
            b, c, s = T // 4, T % 4, T % 2
            PE.need(("v", b, c))
            if c < 3:
                dl = take(("state", T))
                PE.need(("kw", T))
                for h in range(4):
                    PE.do(lambda e, h=h: e.matmul(dl[:, 128 * h:128 * h + 128], kwb[:, 128 * h:128 * h + 128],
                                                  vv[:, c, 128 * h:128 * h + 128], start=True, stop=True),
                          ("dl", T) if h == 3 else None)
            yl = take(("yla", T))
            PE.need(("attn", T))
            for h in range(4):
                PE.do(lambda e, h=h: e.matmul(yl[:, 128 * h:128 * h + 128], att[:, 128 * h:128 * h + 128],
                                              vv[:, c, 128 * h:128 * h + 128], start=True, stop=True),
                      ("yl", T) if h == 3 else None)
            if c >= 1:
                yg = take(("x1", T))
                PE.need(("state", T - 1))
                for h in range(4):
                    PE.do(lambda e, h=h: e.matmul(yg[:, 128 * h:128 * h + 128],
                                                  qT[:, b % 2, h, 128 * c:128 * c + 128],
                                                  st[:, (T - 1) % 2, 128 * h:128 * h + 128], start=True, stop=True),
                          ("yg", T) if h == 3 else None)
            if c < 3:
                DV.need(("dl", T))
                if c == 0:
                    if T >= 4:
                        DV.need(("yg", T - 1))
                    DV.do(lambda e: e.tensor_copy(st[:, s, :], dl[:, :]), ("state", T))
                else:
                    DV.need(("state", T - 1))
                    if T >= 2 and c == 2:
                        DV.need(("yg", T - 1))
                    for h in range(4):
                        hs = slice(128 * h, 128 * h + 128)
                        DV.do(lambda e, h=h, hs=hs: e.scalar_tensor_tensor(
                            st[:, s, hs], st[:, 1 - s, hs], sm[:, TD, 4 * T + h:4 * T + h + 1], dl[:, hs],
                            ALU.mult, ALU.add), ("state", T) if h == 3 else None)
            DV.need(("yl", T))
            DV.do(lambda e: e.tensor_tensor(X1[:, T, :], X1[:, T, :], yl[:, :], ALU.add), ("yla", T))
            DV.need(("yla", T))
            if c >= 1:
                DV.need(("yg", T))
                for h in range(4):
                    hs = slice(128 * h, 128 * h + 128)
                    DV.do(lambda e, h=h, hs=hs: e.scalar_tensor_tensor(
                        X1[:, T, hs], yg[:, hs], sm[:, CD, 4 * T + h:4 * T + h + 1], X1[:, T, hs],
                        ALU.mult, ALU.add), ("x1", T) if h == 3 else None)
            else:
                marks[("x1", T)] = marks[("yla", T)]
            norm_stats("n2", T, X1[:, T, :], [("x1", T)])

        def tail_norm(T):
            war = [("n2", "t", T - 2)] if T >= 2 else [("n1", "t", NT - 2 + T)]
            norm_apply("n2", T, X1[:, T, :], war)

        def tail_turn(T):
            return turn("n2", T, True)

        def pair(i):
            return (PS[2], PS[3]) if i < 12 or i % 2 else (PS[4], PS[5])

        def upgate(i):
            g, b, j = i // 16, (i % 16) // 4, i % 4
            buf = WR[g % 2]
            pg, pu = pair(i)
            if i == 12:
                PE.need(("attn", NT - 1), *freed[5])
            elif i == 13:
                PE.need(("inter", 11))
            elif i >= 12:
                PE.need(("inter", i - 2))
            elif i >= 1:
                PE.need(("inter", i - 1))
            for T in range(4 * b, 4 * b + 4):
                PE.need(("n2", "hi", T), ("n2", "lo", T))
            for o, bank, name in ((0, pg, "gate"), (4, pu, "up")):
                for c in range(2):
                    for nib in range(2):
                        PE.need(("whi", 6 * g + o // 2 + c, nib), ("wlo", 6 * g + o // 2 + c, nib))
                n = 0
                for kt in range(4):
                    for xp, wp in XP:
                        PE.do(lambda e, bank=bank, o=o, kt=kt, xp=xp, wp=wp, n=n: e.matmul(
                            bank[:, :], buf[:, wp, o + kt, 128 * j:128 * j + 128], XT[:, xp, kt, 512 * b:512 * b + 512],
                            start=(n == 0), stop=(n == 11)), (name, i) if n == 11 else None)
                        n += 1

        def gate(i):
            g, b, j = i // 16, (i % 16) // 4, i % 4
            bank, buf = PS[2 + i % 2], WR[g % 2]
            PE.need(*[("inter", 31)] if i < 34 else [("wg", i - 2)])
            for c in range(2):
                for nib in range(2):
                    PE.need(("whi", 6 * g + c, nib), ("wlo", 6 * g + c, nib))
            n = 0
            for kt in range(4):
                for xp, wp in XP:
                    PE.do(lambda e, kt=kt, xp=xp, wp=wp, n=n: e.matmul(
                        bank[:, :], buf[:, wp, kt, 128 * j:128 * j + 128], XT[:, xp, kt, 512 * b:512 * b + 512],
                        start=(n == 0), stop=(n == 11)), ("gate", i) if n == 11 else None)
                    n += 1

        bank_of = {"P1": PS[4][:, 0:256], "P5": PS[5][:, 0:256], "P7": PS[0][:, 0:256], "P6": PS[1][:, 0:256],
                   "P4": PS[5][:, 0:256], "P3": PS[4][:, 0:256], "P2": PS[4][:, 256:512]}

        def up_set(m):
            g, b, u = m // 8, m % 8 // 2, m % 2
            buf = WR[g % 2]
            e0, o0, t0 = 256 * u, 256 * u + 128, 512 * b
            if m == 16:
                PE.need(("inter", 30), *freed[0], *freed[1])
            else:
                PE.need(("C11", m - 1), ("C22", m - 1))
            PE.need(("wlo", 6 * g + 2, 0), ("whi", 6 * g + 3, 1), ("wlo", 6 * g + 3, 1), ("tlo", b, 3))

            def wide(s):
                return lambda wp, kt: WRX[:, g % 2, wp, s, kt, 128 * u:128 * u + 128]

            def left(k, o):
                return lambda wp, kt: buf[:, wp, k + kt, o:o + 128]

            def toks(k, o):
                return lambda xp, kt: XT[:, xp, k + kt, t0 + o:t0 + o + 256]

            def sums(t):
                return lambda xp, kt: TB[b][:, xp, t, kt, :]

            for name, w, x, after in (
                    ("P1", left(4, e0), toks(0, 0), None),
                    ("P5", left(4, o0), sums(0), None),
                    ("P7", wide(1), sums(2), None),
                    ("P6", wide(0), sums(1), None),
                    ("P4", left(6, o0), sums(3), "s5"),
                    ("P3", wide(2), toks(2, 256), "s1"),
                    ("P2", left(6, e0), toks(2, 0), None)):
                bank = bank_of[name]
                if after:
                    PE.need((after, m))
                n = 0
                for kt in range(2):
                    for xp, wp in XP:
                        PE.do(lambda e, bank=bank, w=w, x=x, kt=kt, xp=xp, wp=wp, n=n: e.matmul(
                            bank, w(wp, kt), x(xp, kt), start=(n == 0), stop=(n == 5)), (name, m) if n == 5 else None)
                        n += 1

        GS = 1.0 / (XS * WS)

        def slot(i):
            n, j = i // 4, i % 4
            return ihl_r[:, j] if n >= 3 and n % 2 else ihl_s[:, j]

        def gelu(i, pg):
            w = fw[:, i % 2, :]
            AC.need(("gate", i))
            if i >= 2:
                AC.need(("ilo", i - 2))
            AC.do(lambda e: e.activation(w, pg[:, :], ACT.Square, scale=CUB ** 0.5 * GS), ("sq", i))
            DV.need(("sq", i))
            DV.do(lambda e: e.scalar_tensor_tensor(w, w, 1.0, pg[:, :], ALU.add, ALU.mult), ("pp", i))
            AC.need(("pp", i))
            AC.do(lambda e: e.activation(w, w, ACT.Tanh, scale=GK * GS), ("tanh", i))
            DV.need(("tanh", i))
            DV.do(lambda e: e.scalar_tensor_tensor(w, w, 1.0, pg[:, :], ALU.add, ALU.mult), ("wg", i))
            DV.need(("wg", i))

        def inter(i, pu):
            w = fw[:, i % 2, :]
            DV.do(lambda e: e.scalar_tensor_tensor(w, w, 0.5 * GS * GS * IS, pu, ALU.mult, ALU.mult), ("inter", i))

        def inter_parts(i):
            n = i // 4
            w = fw[:, i % 2, :]
            ih = slot(i)
            AC.need(("inter", i))
            before = n - 1 if n < 3 else (2 if n == 4 else (n - 2 if n > 4 else -1))
            if before >= 0:
                AC.need(("dn", before, 3))
            if n == 3:
                AC.need(("yl", NT - 1))
            AC.do(lambda e: e.copy(ih[:, 0, :], w), ("ihi", i))
            lane = PL if 8 <= i < 15 and i != 11 else DV
            lane.need(("ihi", i))
            lane.do(lambda e: e.tensor_tensor(ih[:, 1, :], w, ih[:, 0, :], ALU.subtract), ("ilo", i))

        def act_tile(i):
            pg, pu = pair(i)
            gelu(i, pg)
            DV.need(("up", i))
            inter(i, pu[:, :])
            inter_parts(i)

        def up_tiles(m):
            ee, oo = 2 * m, 2 * m + 1
            if m == 16:
                AC.need(("tlo", 3, 3))
            else:
                AC.need(("inter", oo - 2), ("inter", ee - 2))
            u2, u3 = ub[:, 0, 256:512], ub[:, 1, 256:512]
            for name, after, dst in (("s1", "P1", ub[:, 0, 0:256]), ("s5", "P5", s5b)):
                AC.need((after, m))
                AC.do(lambda e, dst=dst, src=bank_of[after]: e.copy(dst, src), (name, m))
            for name, after, dst, x, y in (
                    ("U2", [("s1", m), ("P6", m)], u2, ub[:, 0, 0:256], bank_of["P6"]),
                    ("U3", [("U2", m), ("P7", m)], u3, u2, bank_of["P7"]),
                    ("U4", [("U3", m), ("s5", m)], u2, u2, s5b),
                    ("C21", [("U3", m), ("P4", m)], ub[:, 1, 0:256], u3, bank_of["P4"]),
                    ("C22", [("C21", m)], u3, u3, s5b),
                    ("C12", [("U4", m), ("P2", m)], u2, u2, bank_of["P3"]),
                    ("C11", [("s1", m), ("P2", m)], ub[:, 0, 0:256], ub[:, 0, 0:256], bank_of["P2"])):
                DV.need(*after)
                DV.do(lambda e, dst=dst, x=x, y=y: e.tensor_tensor(dst, x, y, ALU.add), (name, m))
                if name == "C22":
                    DV.need(("C22", m))
                    inter(oo, ub[:, 1, :])
            DV.need(("C12", m), ("C11", m))
            inter(ee, ub[:, 0, :])
            inter_parts(oo)
            inter_parts(ee)

        def down(n, tt):
            g, b = n // 4, n % 4
            T = 4 * b + tt
            buf = WR[g % 2]
            bank = take(("ev", n, tt))
            m = 0
            for j in range(4):
                k = 6 * g + 4 + j // 2
                ih = slot(4 * n + j)
                PE.need(("whi", k, j % 2), ("wlo", k, j % 2), ("ilo", 4 * n + j))
                for ip, wp in ((0, 0), (0, 1), (1, 0)):
                    PE.do(lambda e, j=j, ih=ih, ip=ip, wp=wp, m=m: e.matmul(
                        bank[:, :], ih[:, ip, 128 * tt:128 * tt + 128], buf[:, wp, 8 + j, :],
                        start=(m == 0), stop=(m == 11)), ("dn", n, tt) if m == 11 else None)
                    m += 1

            def gather():
                DV.need(("dn", n, tt))
                DV.do(lambda e: e.scalar_tensor_tensor(
                    X1[:, T, :], bank[:, :], 1.0 / (WS * IS), X1[:, T, :], ALU.mult, ALU.add), ("ev", n, tt))
            return gather

        nk = 0

        started = [0]

        def dequant_start(limit):
            if nk == started[0] and nk < min(limit, 48):
                dq_bits(nk)
                started[0] += 1

        def dequant_finish():
            nonlocal nk
            if nk < started[0]:
                if nk >= 12 and nk % 6 in (2, 3):
                    (dq_up0 if nk % 6 == 2 else dq_up1)(nk)
                else:
                    dq_mul(nk)
                if nk + 2 < 48:
                    load_chunk(nk + 2)
                nk += 1

        def dequant(limit):
            dequant_start(limit)
            dequant_finish()

        for k in range(2):
            load_chunk(k)
        lows = {}
        items = [(0, k, h) for k in "kq" for h in range(4)] + [(0, "v", h) for h in range(3)] + [(1,) + KQ[0]]
        nxt = [(1,) + it for it in KQ[1:]]
        def stats1(T):
            norm_stats("n1", T, X1[:, T, :], [("xt", T) if T < 4 else ("x", T // 4)])
            norm_scale("n1", T)

        for T in range(4):
            stats1(T)
            if T >= 1:
                norm_apply("n1", T - 1, X1[:, T - 1, :], [("n1", "t", T - 3)] if T >= 3 else [])
                lows[T - 1] = turn("n1", T - 1, False)
            if T >= 2:
                lows[T - 2]()
        norm_apply("n1", 3, X1[:, 3, :], [("n1", "t", 1)])
        lows[3] = turn("n1", 3, False)
        low = wprep(1)
        lows[2]()
        lows[3]()
        low()
        prep_ab()
        posts = []
        stats1(4)
        for T in range(4, NT):
            if T + 1 < NT:
                stats1(T + 1)
            norm_apply("n1", T, X1[:, T, :], [("n1", "t", T - 2)])
            for f in posts:
                f()
            if T in (5, 9):
                wlow = wprep(0 if T == 5 else 2)
            if 5 <= T < 8:
                wlow([[0, 1], [2], [3]][T - 5])
            if 9 <= T < 11:
                wlow([2 * T - 18, 2 * T - 17])
            posts = [qkv(*items.pop(0))]
            low = turn("n1", T, False)
            logits(T - 4)
            low()
        for f in posts:
            f()
        posts = [qkv(*nxt.pop(0))]
        for T in range(NT - 4, NT):
            logits(T)
        posts.append(qkv(*nxt.pop(0)))
        while items:
            nxt.insert(0, items.pop())
        gates()
        gates_sum()
        for f in posts:
            f()
        decay_rows(0)
        decay_rows(1)
        posts = [qkv(*nxt.pop(0))]
        decay(0)
        decay_mask(0)
        for f in posts:
            f()

        dequant_start(6)

        for T in range(NT):
            b, c = T // 4, T % 4
            i = T - 4
            fill = []
            if b == 0:
                for _ in range(-(-len(nxt) // (4 - c))):
                    fill.append(nxt.pop(0))
            elif b < 3:
                fill += [(b + 1,) + KQ[2 * c], (b + 1,) + KQ[2 * c + 1]]
            if T + 3 < NT:
                fill.append(((T + 3) // 4, "v", (T + 3) % 4))
            kn = head(T, (lambda: norm_scale("n2", T - 1)) if T >= 1 else (lambda: None))
            if T + 1 < NT:
                decay(T + 1)
                decay_mask(T + 1)
            if T + 2 < NT:
                decay_rows(T + 2)
            first = [qkv(*f) for f in fill[:2]]
            if not fill:
                upgate(i)
            low = tail_turn(T - 1) if T >= 1 else None
            if T >= 1:
                tail_norm(T - 1)
            weigh_k(T, kn)
            weigh_s(T)
            for f in first:
                f()
            if low:
                low()
            rest = [qkv(*f) for f in fill[2:]]
            if i > 0 and i % 4 == 0:
                rest += [down(i // 4 - 1, tt) for tt in range(4)]
            for f in rest:
                f()
            if i >= 0:
                if fill:
                    upgate(i)
                act_tile(i)
            if T < 13:
                dequant_finish()
            mid(T)
            if T in (0, 1, 2, 4, 6):
                dequant_start(6)
        norm_scale("n2", NT - 1)
        dequant_start(12)
        dequant_finish()
        g0 = [down(2, tt) for tt in range(3)]
        tail_norm(NT - 1)
        low = tail_turn(NT - 1)
        g0.append(down(2, 3))
        dequant_start(12)
        low()
        for f in g0[:3]:
            f()
        dequant_finish()
        g0[3]()
        ring[:] = [0, 1, 6, 7]

        def dequant_ahead(r):
            base = 6 * (r // 8 + 1)
            if r % 8 == 6 and base < 48:
                dq_up2(base + 3)
            elif r % 8 in (0, 2, 3, 4, 5, 7):
                dequant(48)

        for i in range(12, 32):
            n, j = i // 4, i % 4
            upgate(i)
            f = down(n - 1, j) if n >= 4 else None
            if i == 12:
                dequant_start(12)
            act_tile(i)
            if i in (12, 13):
                dequant_finish()
            if i in (12, 15, 17):
                dequant_start(12)
            if i in (16, 18):
                dequant_finish()
            if 16 <= i < 28:
                pair_sums(i)
            if i >= 20 and i % 2:
                dequant_ahead(i // 2)
            if f:
                f()
        ring[:] = [6, 7]
        for m in range(16, NI // 2):
            ee, oo = 2 * m, 2 * m + 1
            n = ee // 4
            gate(ee)
            gate(oo)
            f = down(n - 1, ee % 4)
            up_set(m)
            h = down(n - 1, oo % 4)
            gelu(ee, PS[2])
            gelu(oo, PS[3])
            f()
            up_tiles(m)
            dequant_ahead(m)
            h()
        for j in range(4):
            down(NI // 4 - 1, j)()
        ov = out.rearrange("(t p) d -> t p d", p=128)
        for T in range(NT):
            SP.need(("ev", NI // 4 - 4 + T // 4, T % 4))
            SP.load(lambda e, T=T: e.dma_start(ov[T], X1[:, T, :]), ("out",), s_o, 16 * NT)
        SP.need(("out",))

        block = ctx.enter_context(nc.Block())

        @block.sync
        def _(eng):
            SP.emit(eng)

        @block.gpsimd
        def _(eng):
            PL.emit(eng)

        @block.scalar
        def _(eng):
            AC.emit(eng)

        @block.vector
        def _(eng):
            DV.emit(eng)

        @block.tensor
        def _(eng):
            PE.emit(eng)


def kernel(**inputs):
    import numpy as np
    import concourse.bacc as bacc
    from concourse.bass_utils import run_bass_kernel_spmd as run

    a = {k[3:]: np.asarray(v) for k, v in inputs.items()}
    n = np.arange(4096).reshape(16, 128, 2).transpose(0, 2, 1).reshape(-1)

    def gu_codes(w):
        return w[n].T.reshape(2, 128, 8, 512).transpose(2, 0, 1, 3)

    def gu_scales(w):
        return w[n].T.reshape(2, 8, 8, 512).transpose(2, 0, 1, 3)

    codes = np.concatenate([gu_codes(a["ffn_gate_W_packed"]), gu_codes(a["ffn_up_W_packed"]),
                            a["ffn_down_W_packed"].T.reshape(8, 2, 128, 512)], axis=1)
    scales = np.concatenate([gu_scales(a["ffn_gate_scales"]), gu_scales(a["ffn_up_scales"]),
                             a["ffn_down_scales"].T.reshape(8, 2, 8, 512)], axis=1)
    arrays = {
        "x": a["attn_x"].reshape(2048, 512),
        "wqkv": np.concatenate([a["attn_Wq"], a["attn_Wk"], a["attn_Wv"]], axis=1),
        "bqk": np.concatenate([a["attn_bq"].reshape(4, 128), a["attn_bk"].reshape(4, 128)]).T,
        "bv": a["attn_bv"].reshape(1, 512),
        "wab": np.concatenate([a["attn_Walpha"], a["attn_Wbeta"]], axis=1),
        "bab": np.concatenate([a["attn_balpha"], a["attn_bbeta"]]).reshape(1, 8),
        "codes": codes,
        "scales": scales,
    }
    arrays = {k: np.ascontiguousarray(v) for k, v in arrays.items()}
    nc = bacc.Bacc("TRN2", target_bir_lowering=False, num_devices=1)
    args = [nc.dram_tensor(k, v.shape, mybir.dt.from_np(v.dtype), kind="ExternalInput").ap() for k, v in arrays.items()]
    out = nc.dram_tensor("y", (2048, 512), F32, kind="ExternalOutput").ap()
    block_kernel(nc, *args, out)
    r = run(nc, [arrays], core_ids=[0])
    return r.results[0]["y"].reshape(4, 512, 512)
```
